# Optimizing a Trainium2 kernel written in Bass

```python
import numpy as np
import jax
import jax.numpy as jnp

def _softmax(x, axis=-1):
    return jax.nn.softmax(x, axis=axis)

def _gelu(x):
    return jax.nn.gelu(x, approximate=True)

def _silu(x):
    return jax.nn.silu(x)

def _sigmoid(x):
    return jax.nn.sigmoid(x)

def _layernorm(x, axis=-1, eps=1e-05):
    m = jnp.mean(x, axis=axis, keepdims=True)
    v = jnp.var(x, axis=axis, keepdims=True)
    return (x - m) / jnp.sqrt(v + eps)

def _scatter_add(tgt, idx, src, axis=0):
    return tgt.at[idx].add(src)

def _segment_sum(src, seg, n):
    return jax.ops.segment_sum(src, seg, n)
kernel_name = 'mk_dlrm_tower_d1_rec_r8_72316b'

def setup_inputs(seed: int=0):
    np.random.seed(seed)
    _w = jnp.asarray

    def _rec_inputs():
        import jax
        import jax.numpy as jnp
        _tk = jax.random.key(seed)
        dense_ctx = jax.random.normal(jax.random.fold_in(_tk, 190), (512, 16), jnp.float32)
        ids = jnp.stack([jax.random.randint(jax.random.fold_in(_tk, 200 + f), (512,), 0, v, jnp.int32) for f, v in enumerate([1250, 1000, 1250, 12500, 1000, 12500, 125000, 12500, 125000, 12500, 12500, 125000, 1000, 1250, 12500, 12500, 1000, 1000, 1250, 1000, 125000, 1250, 12500, 12500, 12500, 1250, 12500, 1000, 1000, 125000, 1000, 125000, 1250, 12500, 12500, 1250, 1250, 12500, 12500, 1000])], axis=1)
        tbl_0 = 0.05 * jax.random.normal(jax.random.fold_in(_tk, 500 + 0), (1250, 32), jnp.float32)
        tbl_1 = 0.05 * jax.random.normal(jax.random.fold_in(_tk, 500 + 1), (1000, 32), jnp.float32)
        tbl_2 = 0.05 * jax.random.normal(jax.random.fold_in(_tk, 500 + 2), (1250, 32), jnp.float32)
        tbl_3 = 0.05 * jax.random.normal(jax.random.fold_in(_tk, 500 + 3), (12500, 32), jnp.float32)
        tbl_4 = 0.05 * jax.random.normal(jax.random.fold_in(_tk, 500 + 4), (1000, 32), jnp.float32)
        tbl_5 = 0.05 * jax.random.normal(jax.random.fold_in(_tk, 500 + 5), (12500, 32), jnp.float32)
        tbl_6 = 0.05 * jax.random.normal(jax.random.fold_in(_tk, 500 + 6), (125000, 32), jnp.float32)
        tbl_7 = 0.05 * jax.random.normal(jax.random.fold_in(_tk, 500 + 7), (12500, 32), jnp.float32)
        tbl_8 = 0.05 * jax.random.normal(jax.random.fold_in(_tk, 500 + 8), (125000, 32), jnp.float32)
        tbl_9 = 0.05 * jax.random.normal(jax.random.fold_in(_tk, 500 + 9), (12500, 32), jnp.float32)
        tbl_10 = 0.05 * jax.random.normal(jax.random.fold_in(_tk, 500 + 10), (12500, 32), jnp.float32)
        tbl_11 = 0.05 * jax.random.normal(jax.random.fold_in(_tk, 500 + 11), (125000, 32), jnp.float32)
        tbl_12 = 0.05 * jax.random.normal(jax.random.fold_in(_tk, 500 + 12), (1000, 32), jnp.float32)
        tbl_13 = 0.05 * jax.random.normal(jax.random.fold_in(_tk, 500 + 13), (1250, 32), jnp.float32)
        tbl_14 = 0.05 * jax.random.normal(jax.random.fold_in(_tk, 500 + 14), (12500, 32), jnp.float32)
        tbl_15 = 0.05 * jax.random.normal(jax.random.fold_in(_tk, 500 + 15), (12500, 32), jnp.float32)
        tbl_16 = 0.05 * jax.random.normal(jax.random.fold_in(_tk, 500 + 16), (1000, 32), jnp.float32)
        tbl_17 = 0.05 * jax.random.normal(jax.random.fold_in(_tk, 500 + 17), (1000, 32), jnp.float32)
        tbl_18 = 0.05 * jax.random.normal(jax.random.fold_in(_tk, 500 + 18), (1250, 32), jnp.float32)
        tbl_19 = 0.05 * jax.random.normal(jax.random.fold_in(_tk, 500 + 19), (1000, 32), jnp.float32)
        tbl_20 = 0.05 * jax.random.normal(jax.random.fold_in(_tk, 500 + 20), (125000, 32), jnp.float32)
        tbl_21 = 0.05 * jax.random.normal(jax.random.fold_in(_tk, 500 + 21), (1250, 32), jnp.float32)
        tbl_22 = 0.05 * jax.random.normal(jax.random.fold_in(_tk, 500 + 22), (12500, 32), jnp.float32)
        tbl_23 = 0.05 * jax.random.normal(jax.random.fold_in(_tk, 500 + 23), (12500, 32), jnp.float32)
        tbl_24 = 0.05 * jax.random.normal(jax.random.fold_in(_tk, 500 + 24), (12500, 32), jnp.float32)
        tbl_25 = 0.05 * jax.random.normal(jax.random.fold_in(_tk, 500 + 25), (1250, 32), jnp.float32)
        tbl_26 = 0.05 * jax.random.normal(jax.random.fold_in(_tk, 500 + 26), (12500, 32), jnp.float32)
        tbl_27 = 0.05 * jax.random.normal(jax.random.fold_in(_tk, 500 + 27), (1000, 32), jnp.float32)
        tbl_28 = 0.05 * jax.random.normal(jax.random.fold_in(_tk, 500 + 28), (1000, 32), jnp.float32)
        tbl_29 = 0.05 * jax.random.normal(jax.random.fold_in(_tk, 500 + 29), (125000, 32), jnp.float32)
        tbl_30 = 0.05 * jax.random.normal(jax.random.fold_in(_tk, 500 + 30), (1000, 32), jnp.float32)
        tbl_31 = 0.05 * jax.random.normal(jax.random.fold_in(_tk, 500 + 31), (125000, 32), jnp.float32)
        tbl_32 = 0.05 * jax.random.normal(jax.random.fold_in(_tk, 500 + 32), (1250, 32), jnp.float32)
        tbl_33 = 0.05 * jax.random.normal(jax.random.fold_in(_tk, 500 + 33), (12500, 32), jnp.float32)
        tbl_34 = 0.05 * jax.random.normal(jax.random.fold_in(_tk, 500 + 34), (12500, 32), jnp.float32)
        tbl_35 = 0.05 * jax.random.normal(jax.random.fold_in(_tk, 500 + 35), (1250, 32), jnp.float32)
        tbl_36 = 0.05 * jax.random.normal(jax.random.fold_in(_tk, 500 + 36), (1250, 32), jnp.float32)
        tbl_37 = 0.05 * jax.random.normal(jax.random.fold_in(_tk, 500 + 37), (12500, 32), jnp.float32)
        tbl_38 = 0.05 * jax.random.normal(jax.random.fold_in(_tk, 500 + 38), (12500, 32), jnp.float32)
        tbl_39 = 0.05 * jax.random.normal(jax.random.fold_in(_tk, 500 + 39), (1000, 32), jnp.float32)
        _rk = jax.random.fold_in(_tk, 7)
        W_top1 = 0.0693375 * jax.random.normal(jax.random.fold_in(_tk, 801), (208, 512), jnp.float32)
        W_top2 = 0.0441942 * jax.random.normal(jax.random.fold_in(_tk, 802), (512, 256), jnp.float32)
        W_top3 = 0.0625 * jax.random.normal(jax.random.fold_in(_tk, 803), (256, 1), jnp.float32)
        b_top1 = jnp.zeros((512,), jnp.float32)
        b_top2 = jnp.zeros((256,), jnp.float32)
        return (dense_ctx, ids, tbl_0, tbl_1, tbl_2, tbl_3, tbl_4, tbl_5, tbl_6, tbl_7, tbl_8, tbl_9, tbl_10, tbl_11, tbl_12, tbl_13, tbl_14, tbl_15, tbl_16, tbl_17, tbl_18, tbl_19, tbl_20, tbl_21, tbl_22, tbl_23, tbl_24, tbl_25, tbl_26, tbl_27, tbl_28, tbl_29, tbl_30, tbl_31, tbl_32, tbl_33, tbl_34, tbl_35, tbl_36, tbl_37, tbl_38, tbl_39, W_top1, b_top1, W_top2, b_top2, W_top3)
    dense_ctx, ids, tbl_0, tbl_1, tbl_2, tbl_3, tbl_4, tbl_5, tbl_6, tbl_7, tbl_8, tbl_9, tbl_10, tbl_11, tbl_12, tbl_13, tbl_14, tbl_15, tbl_16, tbl_17, tbl_18, tbl_19, tbl_20, tbl_21, tbl_22, tbl_23, tbl_24, tbl_25, tbl_26, tbl_27, tbl_28, tbl_29, tbl_30, tbl_31, tbl_32, tbl_33, tbl_34, tbl_35, tbl_36, tbl_37, tbl_38, tbl_39, W_top1, b_top1, W_top2, b_top2, W_top3 = _rec_inputs()

    def _L0_rec_setup():
        import jax, jax.numpy as jnp
        import numpy as np
        B, F0, D = (256, 40, 32)
        LAYER0, LAYER1 = (128, 128)
        key = jax.random.key(seed)
        k1, k2, k3 = jax.random.split(key, 3)
        x = jax.random.normal(k1, (B, F0, D), dtype=jnp.float32)
        W0 = jax.random.normal(k2, (F0, F0, LAYER0), dtype=jnp.float32) * 0.05
        b0 = jnp.zeros((LAYER0,), dtype=jnp.float32)
        W1 = jax.random.normal(k3, (F0, LAYER0 // 2, LAYER1), dtype=jnp.float32) * 0.05
        b1 = jnp.zeros((LAYER1,), dtype=jnp.float32)
        return {'x': x, 'W0': W0, 'b0': b0, 'W1': W1, 'b1': b1}
    _L0_rec_all = _L0_rec_setup()
    _L0_rec_in = {k: v for k, v in _L0_rec_all.items() if k in ('W0', 'b0', 'W1', 'b1')}
    del _L0_rec_all
    return {'dense_ctx': dense_ctx, 'ids': ids, 'tbl_0': tbl_0, 'tbl_1': tbl_1, 'tbl_2': tbl_2, 'tbl_3': tbl_3, 'tbl_4': tbl_4, 'tbl_5': tbl_5, 'tbl_6': tbl_6, 'tbl_7': tbl_7, 'tbl_8': tbl_8, 'tbl_9': tbl_9, 'tbl_10': tbl_10, 'tbl_11': tbl_11, 'tbl_12': tbl_12, 'tbl_13': tbl_13, 'tbl_14': tbl_14, 'tbl_15': tbl_15, 'tbl_16': tbl_16, 'tbl_17': tbl_17, 'tbl_18': tbl_18, 'tbl_19': tbl_19, 'tbl_20': tbl_20, 'tbl_21': tbl_21, 'tbl_22': tbl_22, 'tbl_23': tbl_23, 'tbl_24': tbl_24, 'tbl_25': tbl_25, 'tbl_26': tbl_26, 'tbl_27': tbl_27, 'tbl_28': tbl_28, 'tbl_29': tbl_29, 'tbl_30': tbl_30, 'tbl_31': tbl_31, 'tbl_32': tbl_32, 'tbl_33': tbl_33, 'tbl_34': tbl_34, 'tbl_35': tbl_35, 'tbl_36': tbl_36, 'tbl_37': tbl_37, 'tbl_38': tbl_38, 'tbl_39': tbl_39, 'W_top1': W_top1, 'b_top1': b_top1, 'W_top2': W_top2, 'b_top2': b_top2, 'W_top3': W_top3, 'L0_rec_W0': _L0_rec_in['W0'], 'L0_rec_b0': _L0_rec_in['b0'], 'L0_rec_W1': _L0_rec_in['W1'], 'L0_rec_b1': _L0_rec_in['b1']}

def reference(dense_ctx, ids, tbl_0, tbl_1, tbl_2, tbl_3, tbl_4, tbl_5, tbl_6, tbl_7, tbl_8, tbl_9, tbl_10, tbl_11, tbl_12, tbl_13, tbl_14, tbl_15, tbl_16, tbl_17, tbl_18, tbl_19, tbl_20, tbl_21, tbl_22, tbl_23, tbl_24, tbl_25, tbl_26, tbl_27, tbl_28, tbl_29, tbl_30, tbl_31, tbl_32, tbl_33, tbl_34, tbl_35, tbl_36, tbl_37, tbl_38, tbl_39, W_top1, b_top1, W_top2, b_top2, W_top3, L0_rec_W0, L0_rec_b0, L0_rec_W1, L0_rec_b1):
    import jax
    import jax.numpy as jnp

    def _L0_rec_ref(x, W0, b0, W1, b1):
        import jax, jax.numpy as jnp
        import numpy as np
        B, F0, D = (256, 40, 32)
        LAYER0, LAYER1 = (128, 128)
        h0 = jax.nn.relu(jnp.einsum('bid,bjd,ijs->bsd', x, x, W0) + b0[None, :, None])
        half = LAYER0 // 2
        next_hidden, direct0 = (h0[:, :half, :], h0[:, half:, :])
        direct1 = jax.nn.relu(jnp.einsum('bid,bjd,ijs->bsd', x, next_hidden, W1) + b1[None, :, None])
        result = jnp.concatenate([direct0, direct1], axis=1)
        return jnp.sum(result, axis=-1)
    e = jnp.stack([tbl_0[ids[:, 0]], tbl_1[ids[:, 1]], tbl_2[ids[:, 2]], tbl_3[ids[:, 3]], tbl_4[ids[:, 4]], tbl_5[ids[:, 5]], tbl_6[ids[:, 6]], tbl_7[ids[:, 7]], tbl_8[ids[:, 8]], tbl_9[ids[:, 9]], tbl_10[ids[:, 10]], tbl_11[ids[:, 11]], tbl_12[ids[:, 12]], tbl_13[ids[:, 13]], tbl_14[ids[:, 14]], tbl_15[ids[:, 15]], tbl_16[ids[:, 16]], tbl_17[ids[:, 17]], tbl_18[ids[:, 18]], tbl_19[ids[:, 19]], tbl_20[ids[:, 20]], tbl_21[ids[:, 21]], tbl_22[ids[:, 22]], tbl_23[ids[:, 23]], tbl_24[ids[:, 24]], tbl_25[ids[:, 25]], tbl_26[ids[:, 26]], tbl_27[ids[:, 27]], tbl_28[ids[:, 28]], tbl_29[ids[:, 29]], tbl_30[ids[:, 30]], tbl_31[ids[:, 31]], tbl_32[ids[:, 32]], tbl_33[ids[:, 33]], tbl_34[ids[:, 34]], tbl_35[ids[:, 35]], tbl_36[ids[:, 36]], tbl_37[ids[:, 37]], tbl_38[ids[:, 38]], tbl_39[ids[:, 39]]], axis=1)
    z = _L0_rec_ref(e, L0_rec_W0, L0_rec_b0, L0_rec_W1, L0_rec_b1)
    z = z.reshape(z.shape[0], -1)
    h = jnp.concatenate([z, dense_ctx], axis=1)
    h = jnp.maximum(h @ W_top1 + b_top1, 0.0)
    h = jnp.maximum(h @ W_top2 + b_top2, 0.0)
    y = h @ W_top3
    return y

_drawn_inputs = setup_inputs


def setup_inputs(seed=0):
    import zlib

    import numpy as np

    out = dict(_drawn_inputs(seed))
    spreads = {'b_top1': (0.0, 2.0),
     'b_top2': (0.0, 0.8),
     'L0_rec_b0': (0.0, 0.1),
     'L0_rec_b1': (0.0, 0.1)}
    factors = {'tbl_0': 8.0,
     'tbl_1': 8.0,
     'tbl_2': 8.0,
     'tbl_3': 8.0,
     'tbl_4': 8.0,
     'tbl_5': 8.0,
     'tbl_6': 8.0,
     'tbl_7': 8.0,
     'tbl_8': 8.0,
     'tbl_9': 8.0,
     'tbl_10': 8.0,
     'tbl_11': 8.0,
     'tbl_12': 8.0,
     'tbl_13': 8.0,
     'tbl_14': 8.0,
     'tbl_15': 8.0,
     'tbl_16': 8.0,
     'tbl_17': 8.0,
     'tbl_18': 8.0,
     'tbl_19': 8.0,
     'tbl_20': 8.0,
     'tbl_21': 8.0,
     'tbl_22': 8.0,
     'tbl_23': 8.0,
     'tbl_24': 8.0,
     'tbl_25': 8.0,
     'tbl_26': 8.0,
     'tbl_27': 8.0,
     'tbl_28': 8.0,
     'tbl_29': 8.0,
     'tbl_30': 8.0,
     'tbl_31': 8.0,
     'tbl_32': 8.0,
     'tbl_33': 8.0,
     'tbl_34': 8.0,
     'tbl_35': 8.0,
     'tbl_36': 8.0,
     'tbl_37': 8.0,
     'tbl_38': 8.0,
     'tbl_39': 8.0,
     'L0_rec_W0': 6.28,
     'dense_ctx': 3.925}
    for name, (base, spread) in spreads.items():
        noise = np.random.default_rng([zlib.crc32(name.encode()), seed]).standard_normal(out[name].shape)
        drawn = base * np.exp(spread * noise) if base else spread * noise
        out[name] = jnp.asarray(drawn.astype(out[name].dtype))
    for name, factor in factors.items():
        out[name] = (out[name] * factor).astype(out[name].dtype)
    return out
```

```python
import concourse.bass as bass
import numpy as np
from concourse import mybir
from contextlib import ExitStack

B, F, D = 512, 40, 32
S0, S1 = 128, 128
HALF = S0 // 2
DENSE, N1, N2 = 16, 512, 256
CB = 16
COLS = CB * D
CHUNKS = B // CB
ROWS = CB * F
GATHERS = ROWS // 128
FG = 128 // CB
K0 = 3 * F
T0 = (F // 2 + 1) // 3
T1 = F // 2
SPLIT = 2 * F

L0_STEPS, L1_STEPS = (T0 + 1) // 2, T1 // 2
L0_AT = 5
PER_CHUNK = L0_STEPS + L1_STEPS
BODY = 2 * PER_CHUNK
BODIES = CHUNKS // 2
PRE = L0_STEPS
LEAD = 4
NR, NZ, NH = 2, 4, 7
POOL_STEPS = (1, 3, 5, 7, 9, 11)


def kind_of(k):
    q, r = divmod(k, PER_CHUNK)
    if L0_AT <= r < L0_AT + L0_STEPS:
        return 0, 1 - q, r - L0_AT
    return 1, q, r if r < L0_AT else r - L0_STEPS


def tiles_of(layer, s):
    count = T0 if layer == 0 else T1
    return [t for t in (2 * s, 2 * s + 1) if t < count]


def on_pool(k):
    return k % BODY % PER_CHUNK in POOL_STEPS


def build(nc, idx_in, base_in, table, sel0_in, sel1_in, w0a_in, w0b_in, w1_in, b0_in, b1_in, neg_in,
          dense_in, wt1_in, bt1_in, wt2_in, bt2_in, wt3_in, out):
    f32, f32r, i32, u32 = mybir.dt.float32, mybir.dt.float32r, mybir.dt.int32, mybir.dt.uint32
    ALU, ACT, AX = mybir.AluOpType, mybir.ActivationFunctionType, mybir.AxisListType

    scratch = nc.dram_tensor("gathered_rows", [CHUNKS * GATHERS * 128, D], f32, kind="Internal").ap()

    ctx = ExitStack()
    with ctx:
        def sb(name, shape, dt=f32):
            return ctx.enter_context(nc.sbuf_tensor(name, shape, dt))

        def sem(name):
            return ctx.enter_context(nc.semaphore(name))

        idx_raw = sb("idx_raw", [128, CHUNKS * GATHERS], i32)
        idx_base = sb("idx_base", [128, CHUNKS * GATHERS], i32)
        idx = sb("idx", [128, CHUNKS * GATHERS], i32)
        idx_slot = sb("idx_slot", [128, 2, GATHERS], i32)
        rows = sb("rows", [128, 2, GATHERS * D])
        x3 = sb("x3", [K0, 2, COLS])
        x_high = sb("x_high", [SPLIT, COLS], f32r)
        xs = sb("xs", [SPLIT, 2, COLS], f32r)
        neg = sb("neg", [SPLIT, 1])
        raw0 = sb("raw0", [K0, T0 * S0])
        raw0b = sb("raw0b", [K0, T0 * S0])
        raw1 = sb("raw1", [128, T1 * S1])
        w0h, w0l = sb("w0h", [K0, T0, S0], f32r), sb("w0l", [K0, T0, S0], f32r)
        w1h, w1l = sb("w1h", [128, T1, S1], f32r), sb("w1l", [128, T1, S1], f32r)
        sel_raw = sb("sel_raw", [SPLIT, T1 * 128])
        sel0_raw = sb("sel0_raw", [SPLIT, T0 * K0])
        sel0 = sb("sel0", [SPLIT, T0, K0], f32r)
        sel1 = sb("sel1", [SPLIT, T1, 128], f32r)
        b0, b1 = sb("b0", [128, 1]), sb("b1", [128, 1])
        wt1 = sb("wt1", [128, 2, N1])
        wt2 = sb("wt2", [128, N1 // 128, N2])
        wt3 = sb("wt3", [128, N2 // 128])
        bt1, bt2 = sb("bt1", [128, N1 // 128]), sb("bt2", [128, N2 // 128])
        z = sb("z", [128, NZ, 2, COLS])
        zh = sb("zh", [128, NH, 2, COLS], f32r)
        zl = sb("zl", [128, NH, 2, COLS], f32r)
        h = sb("h", [128, 2, COLS])
        direct0 = sb("direct0", [128, COLS])
        direct1 = sb("direct1", [128, COLS])
        feat = sb("feat", [128, 2, B])
        a1 = sb("a1", [128, N1 // 128, B])
        a2 = sb("a2", [128, N2 // 128, B])
        y = sb("y", [1, B])

        spread = ctx.enter_context(nc.psum_tensor("spread", [128, NR, 2, COLS], f32))
        acc0 = ctx.enter_context(nc.psum_tensor("acc0", [128, COLS], f32))
        acc1 = ctx.enter_context(nc.psum_tensor("acc1", [128, 2, COLS], f32))

        idx_loaded, idx_ready, idx_copied = sem("idx_loaded"), sem("idx_ready"), sem("idx_copied")
        gathered = [sem("gathered_even"), sem("gathered_odd")]
        stored = [sem("stored_even"), sem("stored_odd")]
        x3_loaded = [sem("x3_loaded_even"), sem("x3_loaded_odd")]
        sel_loaded, w0_loaded, w1_loaded, top_loaded = (
            sem("sel_loaded"), sem("w0_loaded"), sem("w1_loaded"), sem("top_loaded"))
        small_loaded = sem("small_loaded")
        sel0_ready, sel1_ready = sem("sel0_ready"), sem("sel1_ready")
        w0_sum, w0_high, w0_ready = sem("w0_sum"), sem("w0_high"), sem("w0_ready")
        w1_high, w1_ready = sem("w1_high"), sem("w1_ready")
        feat_clear = sem("feat_clear")
        high_done, xs_done = sem("high_done"), sem("xs_done")
        spread_done, mul_done, round_done = sem("spread_done"), sem("mul_done"), sem("round_done")
        low_vector, low_pool = sem("low_vector"), sem("low_pool")
        main_done = sem("main_done")
        h_done, direct0_done, direct1_done = sem("h_done"), sem("direct0_done"), sem("direct1_done")
        sum0_done, sum1_done = sem("sum0_done"), sem("sum1_done")
        top_mm, top_act, y_stored = sem("top_mm"), sem("top_act"), sem("y_stored")

        def steps(it, k):
            return BODY * it + (PRE + k + 1)

        def lows(it, k, pool):
            def upto(n):
                return sum(on_pool(j) == pool for j in range(n))
            start = upto(BODY - PRE)
            return upto(BODY) * it + (upto(BODY + k + 1) - start)

        def need(eng, s, value):
            if not isinstance(value, int) or value > 0:
                eng.wait_ge(s, value)

        def need_low(eng, it, k):
            eng.wait_ge(low_pool if on_pool(k) else low_vector, lows(it, k, on_pool(k)))

        def slot(k, n):
            return (PRE + k) % n

        def pair(ap, p, n):
            return ap[0:p, 0:n, :]

        def spread_x(it, k, kind=None):
            layer, q, s = kind or kind_of(k)
            cit = it + 1 if (k >= PER_CHUNK and layer == 0 and kind is None) else it
            tiles = tiles_of(layer, s)
            if s == 0 and layer == 0:
                nc.tensor.wait_ge(xs_done, 2 * cit + (q + 1))
            need(nc.tensor, mul_done, steps(it, k - NR))
            for n, t in enumerate(tiles):
                m = K0 if layer == 0 else 128
                sel = sel0 if layer == 0 else sel1
                mm = nc.tensor.matmul(spread[0:m, slot(k, NR), n, :], sel[:, t, :], xs[:, q, :],
                                      start=True, stop=True)
            mm.then_inc(spread_done, 1)

        def multiply(it, k, kind=None):
            layer, q, s = kind or kind_of(k)
            cit = it + 1 if (k >= PER_CHUNK and layer == 0 and kind is None) else it
            n, p = len(tiles_of(layer, s)), K0 if layer == 0 else 128
            if layer == 1 and s == 0:
                nc.vector.wait_ge(h_done, 2 * (2 * cit + q + 1))
            if k - NZ >= -PRE or not isinstance(it, int) or it > 0:
                need_low(nc.vector, it, k - NZ)
            nc.vector.wait_ge(spread_done, steps(it, k))
            same = (x3 if layer == 0 else h)[0:p, q, :].unsqueeze(1).broadcast_to([p, n, COLS])
            nc.vector.tensor_tensor(z[0:p, slot(k, NZ), 0:n, :], spread[0:p, slot(k, NR), 0:n, :], same,
                                    ALU.mult).then_inc(mul_done, 1)

        def round_high(it, k, kind=None):
            layer, q, s = kind or kind_of(k)
            n, p = len(tiles_of(layer, s)), K0 if layer == 0 else 128
            need(nc.scalar, main_done, steps(it, k - NH))
            nc.scalar.wait_ge(mul_done, steps(it, k))
            nc.scalar.activation(zh[0:p, slot(k, NH), 0:n, :], z[0:p, slot(k, NZ), 0:n, :],
                                 ACT.Copy).then_inc(round_done, 1)

        def subtract(eng, it, k, kind=None):
            layer, q, s = kind or kind_of(k)
            n, p = len(tiles_of(layer, s)), K0 if layer == 0 else 128
            need(eng, main_done, steps(it, k - NH))
            eng.wait_ge(round_done, steps(it, k))
            eng.tensor_tensor(zl[0:p, slot(k, NH), 0:n, :], z[0:p, slot(k, NZ), 0:n, :],
                              zh[0:p, slot(k, NH), 0:n, :].bitcast(f32),
                              ALU.subtract).then_inc(low_pool if on_pool(k) else low_vector, 1)

        def contract(it, k, kind=None):
            layer, q, s = kind or kind_of(k)
            cit = it + 1 if (k >= PER_CHUNK and layer == 0 and kind is None) else it
            tiles = tiles_of(layer, s)
            p, wh, wl = (K0, w0h, w0l) if layer == 0 else (128, w1h, w1l)
            acc = acc0[:, :] if layer == 0 else acc1[:, q, :]
            if s == 0:
                if layer == 0:
                    need(nc.tensor, direct0_done, 2 * cit + q)
                else:
                    need(nc.tensor, direct1_done, 2 * cit + (q - 1))
            need_low(nc.tensor, it, k)
            last = (T0 if layer == 0 else T1) - 1
            for n, t in enumerate(tiles):
                high, low = zh[0:p, slot(k, NH), n, :], zl[0:p, slot(k, NH), n, :]
                nc.tensor.matmul(acc, wh[:, t, :], high, start=(t == 0), stop=False)
                nc.tensor.matmul(acc, wh[:, t, :], low, start=False, stop=False)
                mm = nc.tensor.matmul(acc, wl[:, t, :], high, start=False, stop=(t == last))
            mm.then_inc(main_done, 1)

        def take_indices(cit, q):
            pool = nc.gpsimd
            need(pool, stored[q], 16 * cit)
            col = (cit * 2 + q) * GATHERS
            pool.tensor_copy(idx_slot[:, q, :], idx[:, bass.ds(col, GATHERS)]).then_inc(idx_copied, 1)
            pool.wait_ge(idx_copied, 2 * cit + (q + 1))

        def fetch_rows(q):
            pool = nc.gpsimd
            for g in range(GATHERS):
                pool.indirect_dma_start(rows[:, q, g * D:(g + 1) * D], None, table,
                                        bass.IndirectOffsetOnAxis(ap=idx_slot[:, q, g:g + 1].bitcast(u32), axis=0),
                                        ).then_inc(gathered[q], 16)

        def turn_rows(cit, q):
            sp = nc.sync
            at, rows_in, rows_out = (cit * 2 + q) * GATHERS * 128, 16 * GATHERS * (cit + 1), 16 * (cit + 1)
            chunk = scratch[bass.ds(at, GATHERS * 128), :]
            sp.wait_ge(gathered[q], rows_in)
            sp.dma_start(chunk.rearrange("(g p) d -> p g d", p=128),
                         rows[:, q, :].rearrange("p (g d) -> p g d", d=D)).then_inc(stored[q], 16)
            sp.wait_ge(stored[q], rows_out)
            for copy in range(3):
                sp.dma_start(x3[copy * F:(copy + 1) * F, q, :],
                             chunk.rearrange("(f b) d -> f (b d)", b=CB)).then_inc(x3_loaded[q], 16)

        def split_x_high(cit, q):
            nc.scalar.wait_ge(x3_loaded[q], 48 * (cit + 1))
            need(nc.scalar, xs_done, 2 * cit + q)
            nc.scalar.activation(x_high[:, :], x3[0:SPLIT, q, :], ACT.Copy).then_inc(high_done, 1)

        def split_x(cit, q, reuse=None):
            nc.vector.wait_ge(high_done, 2 * cit + (q + 1))
            if reuse is not None:
                nc.vector.wait_ge(spread_done, reuse)
            nc.vector.scalar_tensor_tensor(xs[:, q, :], x_high[:, :].bitcast(f32), neg[:, 0:1], x3[0:SPLIT, q, :],
                                           ALU.mult, ALU.add).then_inc(xs_done, 1)

        def finish_layer0(cit, q, main, h_free):
            act = nc.scalar
            act.wait_ge(main_done, main)
            if h_free is not None:
                act.wait_ge(mul_done, h_free)
            act.activation(h[0:HALF, q, :], acc0[0:HALF, :], ACT.Relu, bias=b0[0:HALF, :]).then_inc(h_done, 1)
            act.activation(h[HALF:128, q, :], acc0[0:HALF, :], ACT.Relu, bias=b0[0:HALF, :]).then_inc(h_done, 1)
            need(act, sum0_done, 2 * cit + q)
            act.activation(direct0[HALF:128, :], acc0[HALF:128, :], ACT.Relu,
                           bias=b0[HALF:128, :]).then_inc(direct0_done, 1)

        def finish_layer1(cit, q, main):
            act = nc.scalar
            act.wait_ge(main_done, main)
            need(act, sum1_done, 2 * cit + q)
            act.activation(direct1[:, :], acc1[:, q, :], ACT.Relu, bias=b1[:, :]).then_inc(direct1_done, 1)

        def sum_lanes0(cit, q):
            nc.vector.wait_ge(direct0_done, 2 * cit + (q + 1))
            nc.vector.tensor_reduce(feat[HALF:128, 0, bass.ds((cit * 2 + q) * CB, CB)],
                                    direct0[HALF:128, :].rearrange("p (b d) -> p b d", d=D),
                                    AX.X, ALU.add).then_inc(sum0_done, 1)

        def sum_lanes1(cit, q):
            nc.vector.wait_ge(direct1_done, 2 * cit + (q + 1))
            nc.vector.tensor_reduce(feat[:, 1, bass.ds((cit * 2 + q) * CB, CB)],
                                    direct1[:, :].rearrange("p (b d) -> p b d", d=D),
                                    AX.X, ALU.add).then_inc(sum1_done, 1)

        def body_kinds(last):
            if not last:
                return [kind_of(k) for k in range(BODY)]
            return [kind_of(k) for k in range(PER_CHUNK)] + [(1, 1, s) for s in range(L1_STEPS)]

        PRE_KINDS = [(0, 0, s) for s in range(L0_STEPS)]
        L0_END = L0_AT + L0_STEPS - 1

        def tensor_body(it, first=False, last=False):
            kinds = body_kinds(last)
            for k, kind in enumerate(kinds):
                ahead = k + LEAD
                if ahead < len(kinds):
                    spread_x(it, ahead, kinds[ahead] if last and ahead >= PER_CHUNK else None)
                elif not last:
                    follow(it, ahead)
                contract(it, k, kind if last and k >= PER_CHUNK else None)

        def follow(it, ahead):
            layer, q, s = kind_of(ahead - BODY)
            nc.tensor.wait_ge(mul_done, steps(it, ahead - NR))
            for n, t in enumerate(tiles_of(layer, s)):
                mm = nc.tensor.matmul(spread[:, slot(ahead, NR), n, :], sel1[:, t, :], xs[:, q, :],
                                      start=True, stop=True)
            mm.then_inc(spread_done, 1)

        def vector_body(it, first=False, last=False):
            kinds = body_kinds(last)
            for k, kind in enumerate(kinds):
                special = kind if last and k >= PER_CHUNK else None
                multiply(it, k, special)
                if not on_pool(k - 1) and not (k == 0 and first):
                    subtract(nc.vector, it, k - 1, kinds[k - 1] if k and last and k - 1 >= PER_CHUNK else
                             kind_of(BODY - 1) if k == 0 else None)
                c, r = divmod(k, PER_CHUNK)
                if r == 1 and not (first and c == 0 and False):
                    sum_lanes0(it, c)
                if r == 5 and not (first and c == 0):
                    sum_lanes1(it if c == 1 else it - 1, 1 - c)
                if r == 11 and not last:
                    split_x(it + 1, c, steps(it, c * PER_CHUNK + PER_CHUNK - 1))
            if last:
                k = len(kinds) - 1
                if not on_pool(k):
                    subtract(nc.vector, it, k, kinds[k])
                sum_lanes1(it, 1)

        def scalar_body(it, first=False, last=False):
            kinds = body_kinds(last)
            for k, kind in enumerate(kinds):
                round_high(it, k, kind if last and k >= PER_CHUNK else None)
                c, r = divmod(k, PER_CHUNK)
                if r == 3 and not (first and c == 0):
                    finish_layer1(it if c == 1 else it - 1, 1 - c, steps(it, c * PER_CHUNK - 1))
                if r == 9 and not last:
                    split_x_high(it + 1, c)
                if r == L0_END + LEAD and not (last and c == 1):
                    free = steps(it, c * PER_CHUNK - 1) if not (first and c == 0) else None
                    finish_layer0(it if c == 0 else it + 1, 1 - c, steps(it, c * PER_CHUNK + L0_END), free)
            if last:
                finish_layer1(it, 1, steps(it, len(kinds) - 1))

        def pool_body(it, first=False, last=False):
            kinds = body_kinds(last)
            for k, kind in enumerate(kinds):
                c, r = divmod(k, PER_CHUNK)
                if r == POOL_STEPS[0] and not last:
                    take_indices(it + 1, c)
                if on_pool(k):
                    subtract(nc.gpsimd, it, k, kind if last and k >= PER_CHUNK else None)
                if r == POOL_STEPS[0] and not last:
                    fetch_rows(c)

        def sync_body(it, first=False, last=False):
            for c in range(2):
                turn_rows(it + 1, c)

        block = ctx.enter_context(nc.Block())

        @block.sync
        def _(sp):
            sp.dma_start(idx_raw[:, :], idx_in).then_inc(idx_loaded, 16)
            sp.dma_start(idx_base[:, :], base_in).then_inc(idx_loaded, 16)
            sp.dma_start(neg[:, :], neg_in).then_inc(small_loaded, 16)
            sp.dma_start(b0[:, :], b0_in).then_inc(small_loaded, 16)
            sp.dma_start(b1[:, :], b1_in).then_inc(small_loaded, 16)
            sp.dma_start(sel0_raw[:, :], sel0_in).then_inc(sel_loaded, 16)
            sp.dma_start(raw0[:, :], w0a_in).then_inc(w0_loaded, 16)
            sp.dma_start(raw0b[:, :], w0b_in).then_inc(w0_loaded, 16)
            turn_rows(0, 0)
            turn_rows(0, 1)
            sp.wait_ge(feat_clear, 1)
            sp.dma_start(feat[0:DENSE, 0, :], dense_in).then_inc(top_loaded, 16)
            sp.dma_start(wt1[0:DENSE, 0, :], wt1_in[S1 + HALF:S1 + HALF + DENSE, :]).then_inc(top_loaded, 16)
            sp.dma_start(wt1[HALF:128, 0, :], wt1_in[0:HALF, :]).then_inc(top_loaded, 16)
            sp.dma_start(wt1[:, 1, :], wt1_in[HALF:HALF + S1, :]).then_inc(top_loaded, 16)
            sp.dma_start(wt2[:, :, :], wt2_in.rearrange("(t p) n -> p t n", p=128)).then_inc(top_loaded, 16)
            sp.dma_start(wt3[:, :], wt3_in).then_inc(top_loaded, 16)
            sp.dma_start(bt1[:, :], bt1_in).then_inc(top_loaded, 16)
            sp.dma_start(bt2[:, :], bt2_in).then_inc(top_loaded, 16)
            sync_body(0, first=True)
            with sp.Fori(1, BODIES - 1) as it:
                sync_body(it)
            sp.wait_ge(top_act, N1 // 128 + N2 // 128 + 1)
            sp.dma_start(out, y[:, :]).then_inc(y_stored, 16)
            sp.wait_ge(y_stored, 16)

        @block.gpsimd
        def _(pool):
            pool.wait_ge(idx_loaded, 32)
            pool.tensor_tensor(idx[:, :], idx_raw[:, :], idx_base[:, :], ALU.add).then_inc(idx_ready, 1)
            pool.wait_ge(idx_ready, 1)
            for q in range(2):
                take_indices(0, q)
                fetch_rows(q)
            for s in range(PRE):
                if on_pool(s - PRE):
                    subtract(pool, 0, s - PRE, PRE_KINDS[s])
            pool_body(0, first=True)
            with pool.Fori(1, BODIES - 1) as it:
                pool_body(it)
            pool_body(BODIES - 1, last=True)

        @block.scalar
        def _(act):
            act.dma_start(sel_raw[:, :], sel1_in).then_inc(w1_loaded, 16)
            act.dma_start(raw1[:, :], w1_in).then_inc(w1_loaded, 16)
            act.wait_ge(sel_loaded, 16)
            act.activation(sel0[:, :, :].rearrange("p t m -> p (t m)"), sel0_raw[:, :],
                           ACT.Copy).then_inc(sel0_ready, 1)
            act.wait_ge(w0_sum, 1)
            act.activation(w0h[:, :, :].rearrange("p t m -> p (t m)"), raw0[:, :],
                           ACT.Copy).then_inc(w0_high, 1)
            split_x_high(0, 0)
            act.wait_ge(w1_loaded, 32)
            act.activation(w1h[:, :, :].rearrange("p t m -> p (t m)"), raw1[:, :],
                           ACT.Copy).then_inc(w1_high, 1)
            act.activation(sel1[:, :, :].rearrange("p t m -> p (t m)"), sel_raw[:, :],
                           ACT.Copy).then_inc(sel1_ready, 1)
            split_x_high(0, 1)
            for s in range(PRE):
                round_high(0, s - PRE, PRE_KINDS[s])
            act.wait_ge(small_loaded, 48)
            finish_layer0(0, 0, steps(0, -1), None)
            scalar_body(0, first=True)
            with act.Fori(1, BODIES - 1) as it:
                scalar_body(it)
            scalar_body(BODIES - 1, last=True)
            act.wait_ge(top_loaded, 8 * 16)
            for m in range(N1 // 128):
                act.wait_ge(top_mm, m + 1)
                act.activation(a1[:, m, :], spread[:, m // 2, m % 2, :], ACT.Relu,
                               bias=bt1[:, m:m + 1]).then_inc(top_act, 1)
            for m in range(N2 // 128):
                act.wait_ge(top_mm, N1 // 128 + m + 1)
                act.activation(a2[:, m, :], acc1[:, m, :], ACT.Relu, bias=bt2[:, m:m + 1]).then_inc(top_act, 1)
            act.wait_ge(top_mm, N1 // 128 + N2 // 128 + 1)
            act.activation(y[:, :], acc0[0:1, :], ACT.Copy).then_inc(top_act, 1)

        @block.vector
        def _(dve):
            dve.memset(feat[:, :, :], 0.0)
            dve.memset(wt1[:, 0, :], 0.0).then_inc(feat_clear, 1)
            dve.wait_ge(w0_loaded, 32)
            dve.tensor_tensor(raw0[:, :], raw0[:, :], raw0b[:, :], ALU.add).then_inc(w0_sum, 1)
            dve.wait_ge(w0_high, 1)
            dve.tensor_tensor(w0l[:, :, :].rearrange("p t m -> p (t m)"), raw0[:, :],
                              w0h[:, :, :].rearrange("p t m -> p (t m)").bitcast(f32),
                              ALU.subtract).then_inc(w0_ready, 1)
            dve.wait_ge(small_loaded, 48)
            split_x(0, 0)
            dve.wait_ge(w1_high, 1)
            dve.tensor_tensor(w1l[:, :, :].rearrange("p t m -> p (t m)"), raw1[:, :],
                              w1h[:, :, :].rearrange("p t m -> p (t m)").bitcast(f32),
                              ALU.subtract).then_inc(w1_ready, 1)
            split_x(0, 1)
            for s in range(PRE):
                multiply(0, s - PRE, PRE_KINDS[s])
                if s and not on_pool(s - 1 - PRE):
                    subtract(dve, 0, s - 1 - PRE, PRE_KINDS[s - 1])
            if not on_pool(-1):
                subtract(dve, 0, -1, PRE_KINDS[-1])
            vector_body(0, first=True)
            with dve.Fori(1, BODIES - 1) as it:
                vector_body(it)
            vector_body(BODIES - 1, last=True)

        @block.tensor
        def _(pe):
            pe.wait_ge(sel0_ready, 1)
            for s in range(PRE):
                spread_x(0, s - PRE, PRE_KINDS[s])
            pe.wait_ge(w0_ready, 1)
            pe.wait_ge(sel1_ready, 1)
            for k in range(NR):
                spread_x(0, k)
            for s in range(PRE):
                contract(0, s - PRE, PRE_KINDS[s])
            for k in range(NR, LEAD):
                spread_x(0, k)
            pe.wait_ge(w1_ready, 1)
            tensor_body(0, first=True)
            with pe.Fori(1, BODIES - 1) as it:
                tensor_body(it)
            tensor_body(BODIES - 1, last=True)
            pe.wait_ge(top_loaded, 8 * 16)
            pe.wait_ge(sum0_done, CHUNKS)
            pe.wait_ge(sum1_done, CHUNKS)
            for m in range(N1 // 128):
                for t in range(2):
                    mm = pe.matmul(spread[:, m // 2, m % 2, :], wt1[:, t, m * 128:(m + 1) * 128], feat[:, t, :],
                                   start=(t == 0), stop=(t == 1))
                mm.then_inc(top_mm, 1)
            pe.wait_ge(top_act, N1 // 128)
            for m in range(N2 // 128):
                for t in range(N1 // 128):
                    mm = pe.matmul(acc1[:, m, :], wt2[:, t, m * 128:(m + 1) * 128], a1[:, t, :],
                                   start=(t == 0), stop=(t == N1 // 128 - 1))
                mm.then_inc(top_mm, 1)
            pe.wait_ge(top_act, N1 // 128 + N2 // 128)
            for t in range(N2 // 128):
                mm = pe.matmul(acc0[0:1, :], wt3[:, t:t + 1], a2[:, t, :], start=(t == 0),
                               stop=(t == N2 // 128 - 1))
            mm.then_inc(top_mm, 1)


def kernel(**inputs):
    import concourse.bacc as bacc
    from concourse.bass_utils import run_bass_kernel_spmd

    a = {k: np.asarray(v) for k, v in inputs.items()}
    tables = [a[f"tbl_{f}"] for f in range(F)]
    starts = np.concatenate([[0], np.cumsum([t.shape[0] for t in tables])])[:F].astype(np.int32)
    ids = a["ids"].reshape(CHUNKS, CB, GATHERS, FG).transpose(3, 1, 0, 2).reshape(128, CHUNKS * GATHERS)
    base = np.broadcast_to(starts.reshape(1, 1, GATHERS, FG), (CHUNKS, CB, GATHERS, FG))
    base = base.transpose(3, 1, 0, 2).reshape(128, CHUNKS * GATHERS)
    dist = np.arange(3 * T0)
    rot = (np.arange(F)[None, :] + dist[:, None]) % F
    field0 = rot.reshape(T0 * K0)
    field1 = np.repeat(np.arange(F), HALF)
    hot = lambda f: np.tile((f[None, :] == np.arange(F)[:, None]), (2, 1)).astype(np.float32)
    w0 = a["L0_rec_W0"]
    i = np.arange(F)[None, :].repeat(3 * T0, 0)
    w0a = w0[i, rot]
    w0b = w0[rot, i].copy()
    w0b[0] = 0
    w0b[F // 2] = 0
    tiled = lambda w: w.reshape(T0, K0, S0).transpose(1, 0, 2).reshape(K0, T0 * S0)
    w1 = a["L0_rec_W1"].reshape(T1, 128, S1).transpose(1, 0, 2).reshape(128, T1 * S1)
    arrays = {
        "idx": ids, "idx_base": base, "table": np.concatenate(tables, 0),
        "sel0": hot(field0), "sel1": hot(field1), "w0a": tiled(w0a), "w0b": tiled(w0b), "w1": w1,
        "b0": a["L0_rec_b0"].reshape(S0, 1), "b1": a["L0_rec_b1"].reshape(S1, 1),
        "neg": np.repeat(np.float32([0, -1]), F).reshape(SPLIT, 1),
        "dense_t": a["dense_ctx"].T, "w_top1": a["W_top1"], "b_top1": a["b_top1"].reshape(-1, 128).T,
        "w_top2": a["W_top2"], "b_top2": a["b_top2"].reshape(-1, 128).T,
        "w_top3": a["W_top3"].reshape(-1, 128).T,
    }
    nc = bacc.Bacc("TRN2", target_bir_lowering=False, num_devices=1)
    args = []
    for name, value in arrays.items():
        arrays[name] = value = np.ascontiguousarray(value)
        args.append(nc.dram_tensor(f"{name}_dram", value.shape, mybir.dt.from_np(value.dtype), kind="ExternalInput").ap())
    out = nc.dram_tensor("y_out", (1, B), mybir.dt.float32, kind="ExternalOutput").ap()
    build(nc, *args, out)
    result = run_bass_kernel_spmd(nc, [{f"{n}_dram": v for n, v in arrays.items()}], core_ids=[0])
    return result.results[0]["y_out"].reshape(B, 1)
```

```python
import concourse.bass as bass
import numpy as np
from concourse import mybir
from contextlib import ExitStack

B, F, D = 512, 40, 32
S0, S1 = 128, 128
HALF = S0 // 2
DENSE, N1, N2 = 16, 512, 256
CB = 16
COLS = CB * D
CHUNKS = B // CB
ROWS = CB * F
GATHERS = ROWS // 128
FG = 128 // CB
K0 = 3 * F
T0 = (F // 2 + 1) // 3
T1 = F // 2
SPLIT = 2 * F

L0_STEPS, L1_STEPS = (T0 + 1) // 2, T1 // 2
L0_AT = 4
PER_CHUNK = L0_STEPS + L1_STEPS
BODY = 2 * PER_CHUNK
BODIES = CHUNKS // 2
PRE = L0_STEPS
LEAD = 5
NR = 2
NZ = 4
NH = 7
WHO = "PVPVNPVPVPVPNP"
RELU0_AT = 12
RELU1_AT = 3
SUM0_AT = 1
SUM1_AT = 6
SPLIT_HIGH_AT = 11
SPLIT_AT = 13
TAKE_AT = 0


def kind_of(k):
    q, r = divmod(k, PER_CHUNK)
    if L0_AT <= r < L0_AT + L0_STEPS:
        return 0, 1 - q, r - L0_AT
    return 1, q, r if r < L0_AT else r - L0_STEPS


def tiles_of(layer, s):
    count = T0 if layer == 0 else T1
    return [t for t in (2 * s, 2 * s + 1) if t < count]


def who(k):
    return WHO[k % PER_CHUNK]


NATIVES = [k for k in range(BODY) if who(k) == "N"]


def build(nc, idx_in, base_in, table, sel0_in, sel1_in, w0a_in, w0b_in, w1_in, b0_in, b1_in, neg_in,
          dense_in, wt1_in, bt1_in, wt2_in, bt2_in, wt3_in, out):
    f32, f32r, i32, u32 = mybir.dt.float32, mybir.dt.float32r, mybir.dt.int32, mybir.dt.uint32
    ALU, ACT, AX = mybir.AluOpType, mybir.ActivationFunctionType, mybir.AxisListType

    scratch = nc.dram_tensor("gathered_rows", [CHUNKS * GATHERS * 128, D], f32, kind="Internal").ap()

    ctx = ExitStack()
    with ctx:
        def sb(name, shape, dt=f32):
            return ctx.enter_context(nc.sbuf_tensor(name, shape, dt))

        def sem(name):
            return ctx.enter_context(nc.semaphore(name))

        idx_raw = sb("idx_raw", [128, CHUNKS * GATHERS], i32)
        idx_base = sb("idx_base", [128, CHUNKS * GATHERS], i32)
        idx = sb("idx", [128, CHUNKS * GATHERS], i32)
        idx_slot = sb("idx_slot", [128, 2, GATHERS], i32)
        rows = sb("rows", [128, 2, GATHERS * D])
        x3 = sb("x3", [K0, 2, COLS])
        x_high = sb("x_high", [SPLIT, COLS], f32r)
        xs = sb("xs", [SPLIT, 2, COLS], f32r)
        neg = sb("neg", [SPLIT, 1])
        raw0 = sb("raw0", [K0, T0 * S0])
        raw0b = sb("raw0b", [K0, T0 * S0])
        raw1 = sb("raw1", [128, T1 * S1])
        w0h, w0l = sb("w0h", [K0, T0, S0], f32r), sb("w0l", [K0, T0, S0], f32r)
        w1h, w1l = sb("w1h", [128, T1, S1], f32r), sb("w1l", [128, T1, S1], f32r)
        sel_raw = sb("sel_raw", [SPLIT, T1 * 128])
        sel0_raw = sb("sel0_raw", [SPLIT, T0 * K0])
        sel0 = sb("sel0", [SPLIT, T0, K0], f32r)
        sel1 = sb("sel1", [SPLIT, T1, 128], f32r)
        b0, b1 = sb("b0", [128, 1]), sb("b1", [128, 1])
        wt1 = sb("wt1", [128, 2, N1])
        wt2 = sb("wt2", [128, N1 // 128, N2])
        wt3 = sb("wt3", [128, N2 // 128])
        bt1, bt2 = sb("bt1", [128, N1 // 128]), sb("bt2", [128, N2 // 128])
        z = sb("z", [128, NZ, 2, COLS])
        zn = sb("zn", [128, len(NATIVES), 2, COLS])
        zh = sb("zh", [128, NH, 2, COLS], f32r)
        zl = sb("zl", [128, NH, 2, COLS], f32r)
        h = sb("h", [128, 2, COLS])
        direct0 = sb("direct0", [128, COLS])
        direct1 = sb("direct1", [128, COLS])
        feat = sb("feat", [128, 2, B])
        a1 = sb("a1", [128, N1 // 128, B])
        a2 = sb("a2", [128, N2 // 128, B])
        y = sb("y", [1, B])

        spread = ctx.enter_context(nc.psum_tensor("spread", [128, NR, 2, COLS], f32))
        acc0 = ctx.enter_context(nc.psum_tensor("acc0", [128, COLS], f32))
        acc1 = ctx.enter_context(nc.psum_tensor("acc1", [128, 2, COLS], f32))

        idx_loaded, idx_ready, idx_copied = sem("idx_loaded"), sem("idx_ready"), sem("idx_copied")
        gathered = [sem("gathered_even"), sem("gathered_odd")]
        stored = [sem("stored_even"), sem("stored_odd")]
        x3_loaded = [sem("x3_loaded_even"), sem("x3_loaded_odd")]
        sel_loaded, w0_loaded, w1_loaded, top_loaded = (
            sem("sel_loaded"), sem("w0_loaded"), sem("w1_loaded"), sem("top_loaded"))
        small_loaded = sem("small_loaded")
        sel0_ready, sel1_ready = sem("sel0_ready"), sem("sel1_ready")
        w0_sum, w0_high, w0_ready = sem("w0_sum"), sem("w0_high"), sem("w0_ready")
        w1_high, w1_ready = sem("w1_high"), sem("w1_ready")
        feat_clear = sem("feat_clear")
        high_done, xs_done = sem("high_done"), sem("xs_done")
        spread_done, mul_done, round_done = sem("spread_done"), sem("mul_done"), sem("round_done")
        low_vector, low_pool = sem("low_vector"), sem("low_pool")
        main_done = sem("main_done")
        h_done, direct0_done, direct1_done = sem("h_done"), sem("direct0_done"), sem("direct1_done")
        sum0_done, sum1_done = sem("sum0_done"), sem("sum1_done")
        top_mm, top_act, y_stored = sem("top_mm"), sem("top_act"), sem("y_stored")

        def steps(it, k):
            return BODY * it + (PRE + k + 1)

        def count(it, k, names):
            def upto(n):
                return sum(who(j) in names for j in range(n))
            return upto(BODY) * it + (upto(BODY + k + 1) - upto(BODY - PRE))

        def need(eng, s, value):
            if not isinstance(value, int) or value > 0:
                eng.wait_ge(s, value)

        def need_low(eng, it, k):
            eng.wait_ge(low_pool if who(k) == "P" else low_vector, count(it, k, who(k)))

        def product(k, p, n):
            if who(k) == "N":
                return zn[0:p, NATIVES.index(k % BODY), 0:n, :]
            return z[0:p, slot(k, NZ), 0:n, :]

        def slot(k, n):
            return (PRE + k) % n

        def pair(ap, p, n):
            return ap[0:p, 0:n, :]

        def spread_x(it, k, kind=None):
            layer, q, s = kind or kind_of(k % BODY)
            cit = it + 1 if (k >= PER_CHUNK and layer == 0 and kind is None) else it
            tiles = tiles_of(layer, s)
            if s == 0 and layer == 0:
                nc.tensor.wait_ge(xs_done, 2 * cit + (q + 1))
            need(nc.tensor, mul_done, steps(it, k - NR))
            for n, t in enumerate(tiles):
                m = K0 if layer == 0 else 128
                sel = sel0 if layer == 0 else sel1
                mm = nc.tensor.matmul(spread[0:m, slot(k, NR), n, :], sel[:, t, :], xs[:, q, :],
                                      start=True, stop=True)
            mm.then_inc(spread_done, 1)

        def multiply(it, k, kind=None):
            layer, q, s = kind or kind_of(k)
            cit = it + 1 if (k >= PER_CHUNK and layer == 0 and kind is None) else it
            n, p = len(tiles_of(layer, s)), K0 if layer == 0 else 128
            if layer == 1 and s == 0:
                nc.vector.wait_ge(h_done, 2 * (2 * cit + q + 1))
            if who(k) == "N":
                need(nc.vector, main_done, steps(it, k - BODY))
            else:
                last = k - NZ
                while who(last) == "N":
                    last -= NZ
                if last >= -PRE or not isinstance(it, int) or it > 0:
                    need_low(nc.vector, it, last)
            nc.vector.wait_ge(spread_done, steps(it, k))
            same = (x3 if layer == 0 else h)[0:p, q, :].unsqueeze(1).broadcast_to([p, n, COLS])
            nc.vector.tensor_tensor(product(k, p, n), spread[0:p, slot(k, NR), 0:n, :], same,
                                    ALU.mult).then_inc(mul_done, 1)

        def round_high(it, k, kind=None):
            layer, q, s = kind or kind_of(k)
            n, p = len(tiles_of(layer, s)), K0 if layer == 0 else 128
            if who(k) == "N":
                return
            need(nc.scalar, main_done, steps(it, k - NH))
            nc.scalar.wait_ge(mul_done, steps(it, k))
            nc.scalar.activation(zh[0:p, slot(k, NH), 0:n, :], product(k, p, n),
                                 ACT.Copy).then_inc(round_done, 1)

        def subtract(eng, it, k, kind=None):
            layer, q, s = kind or kind_of(k)
            n, p = len(tiles_of(layer, s)), K0 if layer == 0 else 128
            need(eng, main_done, steps(it, k - NH))
            eng.wait_ge(round_done, count(it, k, "VP"))
            eng.tensor_tensor(zl[0:p, slot(k, NH), 0:n, :], product(k, p, n),
                              zh[0:p, slot(k, NH), 0:n, :].bitcast(f32),
                              ALU.subtract).then_inc(low_pool if who(k) == "P" else low_vector, 1)

        def contract(it, k, kind=None):
            layer, q, s = kind or kind_of(k)
            cit = it + 1 if (k >= PER_CHUNK and layer == 0 and kind is None) else it
            tiles = tiles_of(layer, s)
            p, wh, wl = (K0, w0h, w0l) if layer == 0 else (128, w1h, w1l)
            acc = acc0[:, :] if layer == 0 else acc1[:, q, :]
            if s == 0:
                if layer == 0:
                    need(nc.tensor, direct0_done, 2 * cit + q)
                else:
                    need(nc.tensor, direct1_done, 2 * cit + (q - 1))
            last = (T0 if layer == 0 else T1) - 1
            if who(k) == "N":
                nc.tensor.wait_ge(mul_done, steps(it, k))
                w = raw0 if layer == 0 else raw1
                for n, t in enumerate(tiles):
                    mm = nc.tensor.matmul(acc, w[:, t * S0:(t + 1) * S0], product(k, p, 2)[:, n, :],
                                          start=(t == 0), stop=(t == last))
                mm.then_inc(main_done, 1)
                return
            need_low(nc.tensor, it, k)
            for n, t in enumerate(tiles):
                high, low = zh[0:p, slot(k, NH), n, :], zl[0:p, slot(k, NH), n, :]
                nc.tensor.matmul(acc, wh[:, t, :], high, start=(t == 0), stop=False)
                nc.tensor.matmul(acc, wh[:, t, :], low, start=False, stop=False)
                mm = nc.tensor.matmul(acc, wl[:, t, :], high, start=False, stop=(t == last))
            mm.then_inc(main_done, 1)

        def take_indices(cit, q):
            pool = nc.gpsimd
            need(pool, stored[q], 16 * cit)
            col = (cit * 2 + q) * GATHERS
            pool.tensor_copy(idx_slot[:, q, :], idx[:, bass.ds(col, GATHERS)]).then_inc(idx_copied, 1)
            pool.wait_ge(idx_copied, 2 * cit + (q + 1))

        def fetch_rows(q, g):
            nc.gpsimd.indirect_dma_start(rows[:, q, g * D:(g + 1) * D], None, table,
                                         bass.IndirectOffsetOnAxis(ap=idx_slot[:, q, g:g + 1].bitcast(u32), axis=0),
                                         ).then_inc(gathered[q], 16)

        def turn_rows(cit, q):
            sp = nc.sync
            at, rows_in, rows_out = (cit * 2 + q) * GATHERS * 128, 16 * GATHERS * (cit + 1), 16 * (cit + 1)
            chunk = scratch[bass.ds(at, GATHERS * 128), :]
            sp.wait_ge(gathered[q], rows_in)
            sp.dma_start(chunk.rearrange("(g p) d -> p g d", p=128),
                         rows[:, q, :].rearrange("p (g d) -> p g d", d=D)).then_inc(stored[q], 16)
            sp.wait_ge(stored[q], rows_out)
            for copy in range(3):
                sp.dma_start(x3[copy * F:(copy + 1) * F, q, :],
                             chunk.rearrange("(f b) d -> f (b d)", b=CB)).then_inc(x3_loaded[q], 16)

        def split_x_high(cit, q):
            nc.scalar.wait_ge(x3_loaded[q], 48 * (cit + 1))
            need(nc.scalar, xs_done, 2 * cit + q)
            nc.scalar.activation(x_high[:, :], x3[0:SPLIT, q, :], ACT.Copy).then_inc(high_done, 1)

        def split_x(cit, q, reuse=None):
            nc.vector.wait_ge(high_done, 2 * cit + (q + 1))
            if reuse is not None:
                nc.vector.wait_ge(spread_done, reuse)
            nc.vector.scalar_tensor_tensor(xs[:, q, :], x_high[:, :].bitcast(f32), neg[:, 0:1], x3[0:SPLIT, q, :],
                                           ALU.mult, ALU.add).then_inc(xs_done, 1)

        def finish_layer0(cit, q, main, h_free):
            act = nc.scalar
            act.wait_ge(main_done, main)
            if h_free is not None:
                act.wait_ge(mul_done, h_free)
            act.activation(h[0:HALF, q, :], acc0[0:HALF, :], ACT.Relu, bias=b0[0:HALF, :]).then_inc(h_done, 1)
            act.activation(h[HALF:128, q, :], acc0[0:HALF, :], ACT.Relu, bias=b0[0:HALF, :]).then_inc(h_done, 1)
            need(act, sum0_done, 2 * cit + q)
            act.activation(direct0[HALF:128, :], acc0[HALF:128, :], ACT.Relu,
                           bias=b0[HALF:128, :]).then_inc(direct0_done, 1)

        def finish_layer1(cit, q, main):
            act = nc.scalar
            act.wait_ge(main_done, main)
            need(act, sum1_done, 2 * cit + q)
            act.activation(direct1[:, :], acc1[:, q, :], ACT.Relu, bias=b1[:, :]).then_inc(direct1_done, 1)

        def sum_lanes0(cit, q):
            nc.vector.wait_ge(direct0_done, 2 * cit + (q + 1))
            nc.vector.tensor_reduce(feat[HALF:128, 0, bass.ds((cit * 2 + q) * CB, CB)],
                                    direct0[HALF:128, :].rearrange("p (b d) -> p b d", d=D),
                                    AX.X, ALU.add).then_inc(sum0_done, 1)

        def sum_lanes1(cit, q):
            nc.vector.wait_ge(direct1_done, 2 * cit + (q + 1))
            nc.vector.tensor_reduce(feat[:, 1, bass.ds((cit * 2 + q) * CB, CB)],
                                    direct1[:, :].rearrange("p (b d) -> p b d", d=D),
                                    AX.X, ALU.add).then_inc(sum1_done, 1)

        def body_kinds(last):
            if not last:
                return [kind_of(k) for k in range(BODY)]
            return [kind_of(k) for k in range(PER_CHUNK)] + [(1, 1, s) for s in range(L1_STEPS)]

        PRE_KINDS = [(0, 0, s) for s in range(L0_STEPS)]
        L0_END = L0_AT + L0_STEPS - 1

        def tensor_body(it, first=False, last=False):
            kinds = body_kinds(last)
            for k, kind in enumerate(kinds):
                ahead = k + LEAD
                if ahead < len(kinds):
                    spread_x(it, ahead, kinds[ahead] if last and ahead >= PER_CHUNK else None)
                elif not last:
                    spread_x(it, ahead)
                contract(it, k, kind if last and k >= PER_CHUNK else None)

        def vector_body(it, first=False, last=False):
            kinds = body_kinds(last)
            for k, kind in enumerate(kinds):
                special = kind if last and k >= PER_CHUNK else None
                multiply(it, k, special)
                if who(k - 1) == "V" and not (k == 0 and first):
                    subtract(nc.vector, it, k - 1, kinds[k - 1] if k and last and k - 1 >= PER_CHUNK else
                             kind_of(BODY - 1) if k == 0 else None)
                c, r = divmod(k, PER_CHUNK)
                if r == SUM0_AT:
                    sum_lanes0(it, c)
                if r == SUM1_AT and not (first and c == 0):
                    sum_lanes1(it if c == 1 else it - 1, 1 - c)
                if r == SPLIT_AT and not last:
                    split_x(it + 1, c, steps(it, c * PER_CHUNK + PER_CHUNK - 1))
            if last:
                k = len(kinds) - 1
                if who(k) == "V":
                    subtract(nc.vector, it, k, kinds[k])
                sum_lanes1(it, 1)

        def scalar_body(it, first=False, last=False):
            kinds = body_kinds(last)
            for k, kind in enumerate(kinds):
                round_high(it, k, kind if last and k >= PER_CHUNK else None)
                c, r = divmod(k, PER_CHUNK)
                if r == RELU1_AT and not (first and c == 0):
                    finish_layer1(it if c == 1 else it - 1, 1 - c, steps(it, c * PER_CHUNK - 1))
                if r == SPLIT_HIGH_AT and not last:
                    split_x_high(it + 1, c)
                if r == RELU0_AT and not (last and c == 1):
                    free = steps(it, c * PER_CHUNK - 1) if not (first and c == 0) else None
                    finish_layer0(it if c == 0 else it + 1, 1 - c, steps(it, c * PER_CHUNK + L0_END), free)
            if last:
                finish_layer1(it, 1, steps(it, len(kinds) - 1))

        def pool_body(it, first=False, last=False):
            kinds = body_kinds(last)
            for k, kind in enumerate(kinds):
                c, r = divmod(k, PER_CHUNK)
                if r == TAKE_AT and not last:
                    take_indices(it + 1, c)
                if who(k) == "P":
                    subtract(nc.gpsimd, it, k, kind if last and k >= PER_CHUNK else None)
                if TAKE_AT <= r < TAKE_AT + GATHERS and not last:
                    fetch_rows(c, r - TAKE_AT)

        def sync_body(it, first=False, last=False):
            for c in range(2):
                turn_rows(it + 1, c)

        block = ctx.enter_context(nc.Block())

        @block.sync
        def _(sp):
            sp.dma_start(idx_raw[:, :], idx_in).then_inc(idx_loaded, 16)
            sp.dma_start(idx_base[:, :], base_in).then_inc(idx_loaded, 16)
            sp.dma_start(neg[:, :], neg_in).then_inc(small_loaded, 16)
            sp.dma_start(b0[:, :], b0_in).then_inc(small_loaded, 16)
            sp.dma_start(b1[:, :], b1_in).then_inc(small_loaded, 16)
            sp.dma_start(sel0_raw[:, :], sel0_in).then_inc(sel_loaded, 16)
            sp.dma_start(raw0[:, :], w0a_in).then_inc(w0_loaded, 16)
            sp.dma_start(raw0b[:, :], w0b_in).then_inc(w0_loaded, 16)
            turn_rows(0, 0)
            turn_rows(0, 1)
            sp.wait_ge(feat_clear, 1)
            sp.dma_start(feat[0:DENSE, 0, :], dense_in).then_inc(top_loaded, 16)
            sp.dma_start(wt1[0:DENSE, 0, :], wt1_in[S1 + HALF:S1 + HALF + DENSE, :]).then_inc(top_loaded, 16)
            sp.dma_start(wt1[HALF:128, 0, :], wt1_in[0:HALF, :]).then_inc(top_loaded, 16)
            sp.dma_start(wt1[:, 1, :], wt1_in[HALF:HALF + S1, :]).then_inc(top_loaded, 16)
            sp.dma_start(wt2[:, :, :], wt2_in.rearrange("(t p) n -> p t n", p=128)).then_inc(top_loaded, 16)
            sp.dma_start(wt3[:, :], wt3_in).then_inc(top_loaded, 16)
            sp.dma_start(bt1[:, :], bt1_in).then_inc(top_loaded, 16)
            sp.dma_start(bt2[:, :], bt2_in).then_inc(top_loaded, 16)
            sync_body(0, first=True)
            with sp.Fori(1, BODIES - 1) as it:
                sync_body(it)
            sp.wait_ge(top_act, N1 // 128 + N2 // 128 + 1)
            sp.dma_start(out, y[:, :]).then_inc(y_stored, 16)
            sp.wait_ge(y_stored, 16)

        @block.gpsimd
        def _(pool):
            pool.wait_ge(idx_loaded, 32)
            pool.tensor_tensor(idx[:, :], idx_raw[:, :], idx_base[:, :], ALU.add).then_inc(idx_ready, 1)
            pool.wait_ge(idx_ready, 1)
            for q in range(2):
                take_indices(0, q)
                for g in range(GATHERS):
                    fetch_rows(q, g)
            for s in range(PRE):
                if who(s - PRE) == "P":
                    subtract(pool, 0, s - PRE, PRE_KINDS[s])
            pool_body(0, first=True)
            with pool.Fori(1, BODIES - 1) as it:
                pool_body(it)
            pool_body(BODIES - 1, last=True)

        @block.scalar
        def _(act):
            act.dma_start(sel_raw[:, :], sel1_in).then_inc(w1_loaded, 16)
            act.dma_start(raw1[:, :], w1_in).then_inc(w1_loaded, 16)
            act.wait_ge(sel_loaded, 16)
            act.activation(sel0[:, :, :].rearrange("p t m -> p (t m)"), sel0_raw[:, :],
                           ACT.Copy).then_inc(sel0_ready, 1)
            act.wait_ge(w0_sum, 1)
            act.activation(w0h[:, :, :].rearrange("p t m -> p (t m)"), raw0[:, :],
                           ACT.Copy).then_inc(w0_high, 1)
            split_x_high(0, 0)
            act.wait_ge(w1_loaded, 32)
            act.activation(w1h[:, :, :].rearrange("p t m -> p (t m)"), raw1[:, :],
                           ACT.Copy).then_inc(w1_high, 1)
            act.activation(sel1[:, :, :].rearrange("p t m -> p (t m)"), sel_raw[:, :],
                           ACT.Copy).then_inc(sel1_ready, 1)
            split_x_high(0, 1)
            for s in range(PRE):
                round_high(0, s - PRE, PRE_KINDS[s])
            act.wait_ge(small_loaded, 48)
            finish_layer0(0, 0, steps(0, -1), None)
            scalar_body(0, first=True)
            with act.Fori(1, BODIES - 1) as it:
                scalar_body(it)
            scalar_body(BODIES - 1, last=True)
            act.wait_ge(top_loaded, 8 * 16)
            for m in range(N1 // 128):
                act.wait_ge(top_mm, m + 1)
                act.activation(a1[:, m, :], spread[:, m // 2, m % 2, :], ACT.Relu,
                               bias=bt1[:, m:m + 1]).then_inc(top_act, 1)
            for m in range(N2 // 128):
                act.wait_ge(top_mm, N1 // 128 + m + 1)
                act.activation(a2[:, m, :], acc1[:, m, :], ACT.Relu, bias=bt2[:, m:m + 1]).then_inc(top_act, 1)
            act.wait_ge(top_mm, N1 // 128 + N2 // 128 + 1)
            act.activation(y[:, :], acc0[0:1, :], ACT.Copy).then_inc(top_act, 1)

        @block.vector
        def _(dve):
            dve.memset(feat[:, :, :], 0.0)
            dve.memset(wt1[:, 0, :], 0.0).then_inc(feat_clear, 1)
            dve.wait_ge(w0_loaded, 32)
            dve.tensor_tensor(raw0[:, :], raw0[:, :], raw0b[:, :], ALU.add).then_inc(w0_sum, 1)
            dve.wait_ge(w0_high, 1)
            dve.tensor_tensor(w0l[:, :, :].rearrange("p t m -> p (t m)"), raw0[:, :],
                              w0h[:, :, :].rearrange("p t m -> p (t m)").bitcast(f32),
                              ALU.subtract).then_inc(w0_ready, 1)
            dve.wait_ge(small_loaded, 48)
            split_x(0, 0)
            dve.wait_ge(w1_high, 1)
            dve.tensor_tensor(w1l[:, :, :].rearrange("p t m -> p (t m)"), raw1[:, :],
                              w1h[:, :, :].rearrange("p t m -> p (t m)").bitcast(f32),
                              ALU.subtract).then_inc(w1_ready, 1)
            split_x(0, 1)
            for s in range(PRE):
                multiply(0, s - PRE, PRE_KINDS[s])
                if s and who(s - 1 - PRE) == "V":
                    subtract(dve, 0, s - 1 - PRE, PRE_KINDS[s - 1])
            if who(-1) == "V":
                subtract(dve, 0, -1, PRE_KINDS[-1])
            vector_body(0, first=True)
            with dve.Fori(1, BODIES - 1) as it:
                vector_body(it)
            vector_body(BODIES - 1, last=True)

        @block.tensor
        def _(pe):
            pe.wait_ge(sel0_ready, 1)
            for s in range(PRE):
                spread_x(0, s - PRE, PRE_KINDS[s])
            pe.wait_ge(w0_ready, 1)
            pe.wait_ge(sel1_ready, 1)
            for k in range(NR):
                spread_x(0, k)
            for s in range(PRE):
                contract(0, s - PRE, PRE_KINDS[s])
            for k in range(NR, LEAD):
                spread_x(0, k)
            pe.wait_ge(w1_ready, 1)
            tensor_body(0, first=True)
            with pe.Fori(1, BODIES - 1) as it:
                tensor_body(it)
            tensor_body(BODIES - 1, last=True)
            pe.wait_ge(top_loaded, 8 * 16)
            pe.wait_ge(sum0_done, CHUNKS)
            pe.wait_ge(sum1_done, CHUNKS)
            for m in range(N1 // 128):
                for t in range(2):
                    mm = pe.matmul(spread[:, m // 2, m % 2, :], wt1[:, t, m * 128:(m + 1) * 128], feat[:, t, :],
                                   start=(t == 0), stop=(t == 1))
                mm.then_inc(top_mm, 1)
            pe.wait_ge(top_act, N1 // 128)
            for m in range(N2 // 128):
                for t in range(N1 // 128):
                    mm = pe.matmul(acc1[:, m, :], wt2[:, t, m * 128:(m + 1) * 128], a1[:, t, :],
                                   start=(t == 0), stop=(t == N1 // 128 - 1))
                mm.then_inc(top_mm, 1)
            pe.wait_ge(top_act, N1 // 128 + N2 // 128)
            for t in range(N2 // 128):
                mm = pe.matmul(acc0[0:1, :], wt3[:, t:t + 1], a2[:, t, :], start=(t == 0),
                               stop=(t == N2 // 128 - 1))
            mm.then_inc(top_mm, 1)


def kernel(**inputs):
    import concourse.bacc as bacc
    from concourse.bass_utils import run_bass_kernel_spmd

    a = {k: np.asarray(v) for k, v in inputs.items()}
    tables = [a[f"tbl_{f}"] for f in range(F)]
    starts = np.concatenate([[0], np.cumsum([t.shape[0] for t in tables])])[:F].astype(np.int32)
    ids = a["ids"].reshape(CHUNKS, CB, GATHERS, FG).transpose(3, 1, 0, 2).reshape(128, CHUNKS * GATHERS)
    base = np.broadcast_to(starts.reshape(1, 1, GATHERS, FG), (CHUNKS, CB, GATHERS, FG))
    base = base.transpose(3, 1, 0, 2).reshape(128, CHUNKS * GATHERS)
    dist = np.arange(3 * T0)
    rot = (np.arange(F)[None, :] + dist[:, None]) % F
    field0 = rot.reshape(T0 * K0)
    field1 = np.repeat(np.arange(F), HALF)
    hot = lambda f: np.tile((f[None, :] == np.arange(F)[:, None]), (2, 1)).astype(np.float32)
    w0 = a["L0_rec_W0"]
    i = np.arange(F)[None, :].repeat(3 * T0, 0)
    w0a = w0[i, rot]
    w0b = w0[rot, i].copy()
    w0b[0] = 0
    w0b[F // 2] = 0
    tiled = lambda w: w.reshape(T0, K0, S0).transpose(1, 0, 2).reshape(K0, T0 * S0)
    w1 = a["L0_rec_W1"].reshape(T1, 128, S1).transpose(1, 0, 2).reshape(128, T1 * S1)
    arrays = {
        "idx": ids, "idx_base": base, "table": np.concatenate(tables, 0),
        "sel0": hot(field0), "sel1": hot(field1), "w0a": tiled(w0a), "w0b": tiled(w0b), "w1": w1,
        "b0": a["L0_rec_b0"].reshape(S0, 1), "b1": a["L0_rec_b1"].reshape(S1, 1),
        "neg": np.repeat(np.float32([0, -1]), F).reshape(SPLIT, 1),
        "dense_t": a["dense_ctx"].T, "w_top1": a["W_top1"], "b_top1": a["b_top1"].reshape(-1, 128).T,
        "w_top2": a["W_top2"], "b_top2": a["b_top2"].reshape(-1, 128).T,
        "w_top3": a["W_top3"].reshape(-1, 128).T,
    }
    nc = bacc.Bacc("TRN2", target_bir_lowering=False, num_devices=1)
    args = []
    for name, value in arrays.items():
        arrays[name] = value = np.ascontiguousarray(value)
        args.append(nc.dram_tensor(f"{name}_dram", value.shape, mybir.dt.from_np(value.dtype), kind="ExternalInput").ap())
    out = nc.dram_tensor("y_out", (1, B), mybir.dt.float32, kind="ExternalOutput").ap()
    build(nc, *args, out)
    result = run_bass_kernel_spmd(nc, [{f"{n}_dram": v for n, v in arrays.items()}], core_ids=[0])
    return result.results[0]["y_out"].reshape(B, 1)
```

```python
import concourse.bass as bass
import numpy as np
from concourse import mybir
from contextlib import ExitStack

B, F, D = 512, 40, 32
S0, S1 = 128, 128
HALF = S0 // 2
DENSE, N1, N2 = 16, 512, 256
CB = 16
COLS = CB * D
CHUNKS = B // CB
ROWS = CB * F
GATHERS = ROWS // 128
FG = 128 // CB
K0 = 3 * F
T0 = (F // 2 + 1) // 3
T1 = F // 2
SPLIT = 2 * F

L0_STEPS, L1_STEPS = (T0 + 1) // 2, T1 // 2
L0_AT = 4
PER_CHUNK = L0_STEPS + L1_STEPS
BODY = 2 * PER_CHUNK
BODIES = CHUNKS // 2
PRE = L0_STEPS
LEAD = 5
NR = 2
NZ = 4
NH = 7
WHO = "PNPNVNPNVPPPNP"
NN = 5
BY_DMA = (0, 1, 2, 3, 8, 9, 10, 11)
ND = 4
DMA_LEAD = 6
RELU0_AT = 11
RELU1_AT = 3
SUM0_AT = 1
SUM1_AT = 5
SPLIT_HIGH_AT = 12
SPLIT_AT = 13
TURN_AT = 9
TAKE_AT = 0


def kind_of(k):
    q, r = divmod(k, PER_CHUNK)
    if L0_AT <= r < L0_AT + L0_STEPS:
        return 0, 1 - q, r - L0_AT
    return 1, q, r if r < L0_AT else r - L0_STEPS


def tiles_of(layer, s):
    count = T0 if layer == 0 else T1
    return [t for t in (2 * s, 2 * s + 1) if t < count]


def who(it, k):
    return "N" if isinstance(it, int) and it == 0 and k < 0 else WHO[k % PER_CHUNK]


def by_dma(k):
    return k >= 0 and k % PER_CHUNK in BY_DMA


SPREADS = [k for k in range(BODY) if not by_dma(k)]
DMAS = [k for k in range(BODY) if by_dma(k)]
assert not any(L0_AT <= r < L0_AT + L0_STEPS or r >= PER_CHUNK - NR for r in BY_DMA)
assert len(SPREADS) % NR == 0 and len(DMAS) % ND == 0
NATIVES = [k for k in range(BODY) if who(1, k) == "N"]
assert len(NATIVES) % NN == 0
assert WHO[TAKE_AT] == "P"


def build(nc, idx_in, base_in, table, sel0_in, sel1_in, w0a_in, w0b_in, w1_in, b0_in, b1_in, neg_in,
          dense_in, wt1_in, bt1_in, wt2_in, bt2_in, wt3_in, out):
    f32, f32r = mybir.dt.float32, mybir.dt.float32r
    i32, u32 = mybir.dt.int32, mybir.dt.uint32
    ALU, ACT, AX = mybir.AluOpType, mybir.ActivationFunctionType, mybir.AxisListType

    scratch = nc.dram_tensor("gathered_rows", [CHUNKS * GATHERS * 128, D], f32, kind="Internal").ap()

    ctx = ExitStack()
    with ctx:
        def sb(name, shape, dt=f32):
            return ctx.enter_context(nc.sbuf_tensor(name, shape, dt))

        def sem(name):
            return ctx.enter_context(nc.semaphore(name))

        idx_raw = sb("idx_raw", [128, CHUNKS * GATHERS], i32)
        idx_base = sb("idx_base", [128, CHUNKS * GATHERS], i32)
        idx = sb("idx", [128, CHUNKS * GATHERS], i32)
        idx_slot = sb("idx_slot", [128, 2, GATHERS], i32)
        rows = sb("rows", [128, 2, GATHERS * D])
        x3 = sb("x3", [K0, 2, COLS])
        x_high = sb("x_high", [SPLIT, COLS], f32r)
        xs = sb("xs", [SPLIT, 2, COLS], f32r)
        neg = sb("neg", [SPLIT, 1])
        raw0 = sb("raw0", [K0, T0 * S0])
        raw1 = sb("raw1", [128, T1 * S1])
        w0h, w0l = sb("w0h", [K0, T0, S0], f32r), sb("w0l", [K0, T0, S0], f32r)
        w1h, w1l = sb("w1h", [128, T1, S1], f32r), sb("w1l", [128, T1, S1], f32r)
        sel0 = sb("sel0", [SPLIT, T0, K0], f32r)
        sel1 = sb("sel1", [SPLIT, T1, 128], f32r)
        b0, b1 = sb("b0", [128, 1]), sb("b1", [128, 1])
        wt1 = sb("wt1", [128, 2, N1])
        wt2 = sb("wt2", [128, N1 // 128, N2])
        wt3 = sb("wt3", [128, N2 // 128])
        bt1, bt2 = sb("bt1", [128, N1 // 128]), sb("bt2", [128, N2 // 128])
        z = sb("z", [128, NZ, 2, COLS])
        zn = sb("zn", [128, NN, 2, COLS])
        zh = sb("zh", [128, NH, 2, COLS], f32r)
        zl = sb("zl", [128, NH, 2, COLS], f32r)
        h = sb("h", [128, 2, COLS])
        direct0 = sb("direct0", [128, COLS])
        direct1 = sb("direct1", [128, COLS])
        feat = sb("feat", [128, 2, B])
        sel0_raw = zn[0:SPLIT, 0, :, :].rearrange("p a n -> p (a n)")[:, 0:T0 * K0]
        sel1_raw = z[0:SPLIT, 1:NZ, :, :].rearrange("p s a n -> p (s a n)")[:, 0:T1 * 128]
        raw0b = z[0:K0, 0, :, :].rearrange("p a n -> p (a n)")[:, 0:T0 * S0]
        a1 = z[:, 0:2, :, :].rearrange("p a b n -> p (a b) n")
        a2 = z[:, 2, :, :]
        y = sb("y", [128, B // 128])

        xd = sb("xd", [128, ND, 2, COLS])
        spread = ctx.enter_context(nc.psum_tensor("spread", [128, NR, 2, COLS], f32))
        acc0 = ctx.enter_context(nc.psum_tensor("acc0", [128, COLS], f32))
        acc1 = ctx.enter_context(nc.psum_tensor("acc1", [128, 2, COLS], f32))

        idx_loaded, idx_ready, idx_copied = sem("idx_loaded"), sem("idx_ready"), sem("idx_copied")
        gathered = [sem("gathered_even"), sem("gathered_odd")]
        stored = [sem("stored_even"), sem("stored_odd")]
        x3_loaded = [sem("x3_loaded_even"), sem("x3_loaded_odd")]
        sel_loaded, w0_loaded, w1_loaded, top_loaded = (
            sem("sel_loaded"), sem("w0_loaded"), sem("w1_loaded"), sem("top_loaded"))
        small_loaded = sem("small_loaded")
        sel0_ready, sel1_ready = sem("sel0_ready"), sem("sel1_ready")
        w0_sum, w0_high, w0_ready = sem("w0_sum"), sem("w0_high"), sem("w0_ready")
        w1_high, w1_ready = sem("w1_high"), sem("w1_ready")
        feat_clear = sem("feat_clear")
        xd_loaded = [sem(f"xd_loaded_{n}") for n in range(ND)]
        high_done, xs_done = sem("high_done"), sem("xs_done")
        spread_done, mul_done, round_done = sem("spread_done"), sem("mul_done"), sem("round_done")
        low_vector, low_pool = sem("low_vector"), sem("low_pool")
        main_done = sem("main_done")
        h_done, direct0_done, direct1_done = sem("h_done"), sem("direct0_done"), sem("direct1_done")
        sum0_done, sum1_done = sem("sum0_done"), sem("sum1_done")
        top_mm, top_act, y_stored = sem("top_mm"), sem("top_act"), sem("y_stored")

        def steps(it, k):
            return BODY * it + (PRE + k + 1)

        def count(it, k, names):
            def upto(n):
                return sum(who(1, j) in names for j in range(n))
            return upto(BODY) * it + (upto(BODY + k + 1) - upto(BODY))

        def need(eng, s, value):
            if not isinstance(value, int) or value > 0:
                eng.wait_ge(s, value)

        def need_low(eng, it, k):
            eng.wait_ge(low_pool if who(it, k) == "P" else low_vector, count(it, k, who(it, k)))

        def spreads(it, k):
            if k < 0:
                return len(SPREADS) * it + (PRE + k + 1 if isinstance(it, int) and it == 0 else
                                            PRE - sum(j > k + BODY for j in SPREADS))
            whole, k = divmod(k, BODY)
            return len(SPREADS) * (it + whole) + (PRE + sum(j <= k for j in SPREADS))

        def spread_slot(k):
            return (k if k < 0 else sum(j < k % BODY for j in SPREADS)) % NR

        def spread_before(k):
            if k < 0:
                return k - NR
            at = SPREADS.index(k % BODY) - NR
            return SPREADS[at] + (k - k % BODY) - (BODY if at < 0 else 0)

        def dma_use(it, k):
            at = DMAS.index(k)
            return at % ND, 32 * (len(DMAS) // ND) * it + 32 * (at // ND + 1)

        def native_slot(it, k):
            return (PRE + k if isinstance(it, int) and it == 0 and k < 0 else NATIVES.index(k % BODY)) % NN

        def native_before(it, k):
            if isinstance(it, int) and it == 0 and k < 0:
                return k - NN
            at = NATIVES.index(k) - NN
            if at < 0 and isinstance(it, int) and it == 0:
                return max([j for j in range(-PRE, 0) if (PRE + j) % NN == at % NN], default=-BODY)
            return NATIVES[at] - (BODY if at < 0 else 0)

        def product(it, k, p, n):
            if who(it, k) == "N":
                return zn[0:p, native_slot(it, k), 0:n, :]
            return z[0:p, slot(k, NZ), 0:n, :]

        def slot(k, n):
            return (PRE + k) % n

        def spread_x(it, k, kind=None):
            if by_dma(k % BODY if k >= 0 else k):
                return
            layer, q, s = kind or kind_of(k % BODY)
            cit = it + 1 if (k >= PER_CHUNK and layer == 0 and kind is None) else it
            tiles = tiles_of(layer, s)
            if s == 0 and layer == 0:
                nc.tensor.wait_ge(xs_done, 2 * cit + (q + 1))
            need(nc.tensor, mul_done, steps(it, spread_before(k)))
            for n, t in enumerate(tiles):
                m = K0 if layer == 0 else 128
                sel = sel0 if layer == 0 else sel1
                mm = nc.tensor.matmul(spread[0:m, spread_slot(k), n, :], sel[:, t, :], xs[:, q, :],
                                      start=True, stop=True)
            mm.then_inc(spread_done, 1)

        def multiply(it, k, kind=None):
            layer, q, s = kind or kind_of(k)
            cit = it + 1 if (k >= PER_CHUNK and layer == 0 and kind is None) else it
            n, p = len(tiles_of(layer, s)), K0 if layer == 0 else 128
            if layer == 1 and s == 0:
                nc.vector.wait_ge(h_done, 2 * (2 * cit + q + 1))
            if who(it, k) == "N":
                need(nc.vector, main_done, steps(it, native_before(it, k)))
            else:
                last = k - NZ
                begun = isinstance(it, int) and it == 0
                while who(it, last) == "N" and not (begun and last < 0):
                    last -= NZ
                if not (begun and last < 0):
                    need_low(nc.vector, it, last)
            if by_dma(k):
                at, ready = dma_use(it, k)
                nc.vector.wait_ge(xd_loaded[at], ready)
                x = xd[0:p, at, 0:n, :]
            else:
                nc.vector.wait_ge(spread_done, spreads(it, k))
                x = spread[0:p, spread_slot(k), 0:n, :]
            same = (x3 if layer == 0 else h)[0:p, q, :].unsqueeze(1).broadcast_to([p, n, COLS])
            nc.vector.tensor_tensor(product(it, k, p, n), x, same,
                                    ALU.mult).then_inc(mul_done, 1)

        def spread_by_dma(it, k, kind=None):
            layer, q, s = kind or kind_of(k)
            at, _ = dma_use(it, k)
            before = DMAS.index(k) - ND
            if before >= 0 or not isinstance(it, int) or it > 0:
                nc.sync.wait_ge(mul_done, steps(it, DMAS[before] - (BODY if before < 0 else 0)))
            chunk = scratch[bass.ds((it * 2 + q) * GATHERS * 128, GATHERS * 128), :].rearrange(
                "(f b) d -> f (b d)", b=CB)
            first, n = tiles_of(layer, s)[0], len(tiles_of(layer, s))
            for i in range(2):
                field = chunk[2 * first + i:2 * first + i + 2 * n - 1:2, :].unsqueeze(0)
                nc.sync.dma_start(xd[HALF * i:HALF * (i + 1), at, :, :],
                                  field.broadcast_to([HALF, n, COLS])).then_inc(xd_loaded[at], 16)

        def round_high(it, k, kind=None):
            layer, q, s = kind or kind_of(k)
            n, p = len(tiles_of(layer, s)), K0 if layer == 0 else 128
            if who(it, k) == "N":
                return
            need(nc.scalar, main_done, steps(it, k - NH))
            nc.scalar.wait_ge(mul_done, steps(it, k))
            nc.scalar.activation(zh[0:p, slot(k, NH), 0:n, :], product(it, k, p, n),
                                 ACT.Copy).then_inc(round_done, 1)

        def subtract(eng, it, k, kind=None):
            layer, q, s = kind or kind_of(k)
            n, p = len(tiles_of(layer, s)), K0 if layer == 0 else 128
            need(eng, main_done, steps(it, k - NH))
            eng.wait_ge(round_done, count(it, k, "VP"))
            eng.tensor_tensor(zl[0:p, slot(k, NH), 0:n, :], product(it, k, p, n),
                              zh[0:p, slot(k, NH), 0:n, :].bitcast(f32),
                              ALU.subtract).then_inc(low_pool if who(it, k) == "P" else low_vector, 1)

        def contract(it, k, kind=None):
            layer, q, s = kind or kind_of(k)
            cit = it + 1 if (k >= PER_CHUNK and layer == 0 and kind is None) else it
            tiles = tiles_of(layer, s)
            p, wh, wl = (K0, w0h, w0l) if layer == 0 else (128, w1h, w1l)
            acc = acc0[:, :] if layer == 0 else acc1[:, q, :]
            if s == 0:
                if layer == 0:
                    need(nc.tensor, direct0_done, 2 * cit + q)
                else:
                    need(nc.tensor, direct1_done, 2 * cit + (q - 1))
            last = (T0 if layer == 0 else T1) - 1
            if who(it, k) == "N":
                nc.tensor.wait_ge(mul_done, steps(it, k))
                w = raw0 if layer == 0 else raw1
                for n, t in enumerate(tiles):
                    mm = nc.tensor.matmul(acc, w[:, t * S0:(t + 1) * S0], product(it, k, p, 2)[:, n, :],
                                          start=(t == 0), stop=(t == last))
                mm.then_inc(main_done, 1)
                return
            need_low(nc.tensor, it, k)
            for n, t in enumerate(tiles):
                high, low = zh[0:p, slot(k, NH), n, :], zl[0:p, slot(k, NH), n, :]
                nc.tensor.matmul(acc, wh[:, t, :], high, start=(t == 0), stop=False)
                nc.tensor.matmul(acc, wh[:, t, :], low, start=False, stop=False)
                mm = nc.tensor.matmul(acc, wl[:, t, :], high, start=False, stop=(t == last))
            mm.then_inc(main_done, 1)

        def take_indices(cit, q):
            pool = nc.gpsimd
            need(pool, stored[q], 16 * cit)
            col = (cit * 2 + q) * GATHERS
            pool.tensor_copy(idx_slot[:, q, :], idx[:, bass.ds(col, GATHERS)]).then_inc(idx_copied, 1)
            pool.wait_ge(idx_copied, 2 * cit + (q + 1))

        def fetch_rows(q, g):
            nc.gpsimd.indirect_dma_start(rows[:, q, g * D:(g + 1) * D], None, table,
                                         bass.IndirectOffsetOnAxis(ap=idx_slot[:, q, g:g + 1].bitcast(u32), axis=0),
                                         ).then_inc(gathered[q], 16)

        def turn_rows(cit, q):
            sp = nc.sync
            at, rows_in, rows_out = (cit * 2 + q) * GATHERS * 128, 16 * GATHERS * (cit + 1), 16 * (cit + 1)
            chunk = scratch[bass.ds(at, GATHERS * 128), :]
            sp.wait_ge(gathered[q], rows_in)
            sp.dma_start(chunk.rearrange("(g p) d -> p g d", p=128),
                         rows[:, q, :].rearrange("p (g d) -> p g d", d=D)).then_inc(stored[q], 16)
            sp.wait_ge(stored[q], rows_out)
            for copy in range(3):
                sp.dma_start(x3[copy * F:(copy + 1) * F, q, :],
                             chunk.rearrange("(f b) d -> f (b d)", b=CB)).then_inc(x3_loaded[q], 16)

        def split_x_high(cit, q):
            nc.scalar.wait_ge(x3_loaded[q], 48 * (cit + 1))
            need(nc.scalar, xs_done, 2 * cit + q)
            nc.scalar.activation(x_high[:, :], x3[0:SPLIT, q, :], ACT.Copy).then_inc(high_done, 1)

        def split_x(cit, q, reuse=None):
            nc.vector.wait_ge(high_done, 2 * cit + (q + 1))
            if reuse is not None:
                nc.vector.wait_ge(spread_done, reuse)
            nc.vector.scalar_tensor_tensor(xs[:, q, :], x_high[:, :].bitcast(f32), neg[:, 0:1], x3[0:SPLIT, q, :],
                                           ALU.mult, ALU.add).then_inc(xs_done, 1)

        def finish_layer0(cit, q, main, h_free):
            act = nc.scalar
            act.wait_ge(main_done, main)
            if h_free is not None:
                act.wait_ge(mul_done, h_free)
            act.activation(h[0:HALF, q, :], acc0[0:HALF, :], ACT.Relu, bias=b0[0:HALF, :]).then_inc(h_done, 1)
            act.activation(h[HALF:128, q, :], acc0[0:HALF, :], ACT.Relu, bias=b0[0:HALF, :]).then_inc(h_done, 1)
            need(act, sum0_done, 2 * cit + q)
            act.activation(direct0[HALF:128, :], acc0[HALF:128, :], ACT.Relu,
                           bias=b0[HALF:128, :]).then_inc(direct0_done, 1)

        def finish_layer1(cit, q, main):
            act = nc.scalar
            act.wait_ge(main_done, main)
            need(act, sum1_done, 2 * cit + q)
            act.activation(direct1[:, :], acc1[:, q, :], ACT.Relu, bias=b1[:, :]).then_inc(direct1_done, 1)

        def sum_lanes0(cit, q):
            nc.vector.wait_ge(direct0_done, 2 * cit + (q + 1))
            nc.vector.tensor_reduce(feat[HALF:128, 0, bass.ds((cit * 2 + q) * CB, CB)],
                                    direct0[HALF:128, :].rearrange("p (b d) -> p b d", d=D),
                                    AX.X, ALU.add).then_inc(sum0_done, 1)

        def sum_lanes1(cit, q):
            nc.vector.wait_ge(direct1_done, 2 * cit + (q + 1))
            nc.vector.tensor_reduce(feat[:, 1, bass.ds((cit * 2 + q) * CB, CB)],
                                    direct1[:, :].rearrange("p (b d) -> p b d", d=D),
                                    AX.X, ALU.add).then_inc(sum1_done, 1)

        def body_kinds(last):
            if not last:
                return [kind_of(k) for k in range(BODY)]
            return [kind_of(k) for k in range(PER_CHUNK)] + [(1, 1, s) for s in range(L1_STEPS)]

        PRE_KINDS = [(0, 0, s) for s in range(L0_STEPS)]
        L0_END = L0_AT + L0_STEPS - 1

        def tensor_body(it, last=False):
            kinds = body_kinds(last)
            for k, kind in enumerate(kinds):
                ahead = k + LEAD
                if ahead < len(kinds):
                    spread_x(it, ahead, kinds[ahead] if last and ahead >= PER_CHUNK else None)
                elif not last:
                    spread_x(it, ahead)
                contract(it, k, kind if last and k >= PER_CHUNK else None)

        def vector_body(it, first=False, last=False):
            kinds = body_kinds(last)
            for k, kind in enumerate(kinds):
                special = kind if last and k >= PER_CHUNK else None
                multiply(it, k, special)
                if who(it, k - 1) == "V" and not (k == 0 and first):
                    subtract(nc.vector, it, k - 1, kinds[k - 1] if k and last and k - 1 >= PER_CHUNK else
                             kind_of(BODY - 1) if k == 0 else None)
                c, r = divmod(k, PER_CHUNK)
                if r == SUM0_AT:
                    sum_lanes0(it, c)
                if r == SUM1_AT and not (first and c == 0):
                    sum_lanes1(it if c == 1 else it - 1, 1 - c)
                if r == SPLIT_AT and not last:
                    split_x(it + 1, c, spreads(it, c * PER_CHUNK + PER_CHUNK - 1))
            if last:
                k = len(kinds) - 1
                if who(it, k) == "V":
                    subtract(nc.vector, it, k, kinds[k])
                sum_lanes1(it, 1)

        def scalar_body(it, first=False, last=False):
            kinds = body_kinds(last)
            for k, kind in enumerate(kinds):
                round_high(it, k, kind if last and k >= PER_CHUNK else None)
                c, r = divmod(k, PER_CHUNK)
                if r == RELU1_AT and not (first and c == 0):
                    finish_layer1(it if c == 1 else it - 1, 1 - c, steps(it, c * PER_CHUNK - 1))
                if r == SPLIT_HIGH_AT and not last:
                    split_x_high(it + 1, c)
                if r == RELU0_AT and not (last and c == 1):
                    free = steps(it, c * PER_CHUNK - 1) if not (first and c == 0) else None
                    finish_layer0(it if c == 0 else it + 1, 1 - c, steps(it, c * PER_CHUNK + L0_END), free)
            if last:
                finish_layer1(it, 1, steps(it, len(kinds) - 1))

        def pool_body(it, last=False):
            kinds = body_kinds(last)
            for k, kind in enumerate(kinds):
                c, r = divmod(k, PER_CHUNK)
                if r == TAKE_AT and not last:
                    take_indices(it + 1, c)
                if who(it, k) == "P":
                    subtract(nc.gpsimd, it, k, kind if last and k >= PER_CHUNK else None)
                if TAKE_AT <= r < TAKE_AT + GATHERS and not last:
                    fetch_rows(c, r - TAKE_AT)

        def sync_body(it, last=False):
            kinds = body_kinds(last)
            for k, kind in enumerate(kinds):
                c, r = divmod(k, PER_CHUNK)
                if r == TURN_AT and not last:
                    turn_rows(it + 1, c)
                ahead = k + DMA_LEAD
                if ahead < len(kinds) and by_dma(ahead):
                    spread_by_dma(it, ahead, kinds[ahead])
                elif ahead >= BODY and by_dma(ahead - BODY) and not last:
                    spread_by_dma(it + 1, ahead - BODY)

        block = ctx.enter_context(nc.Block())

        @block.sync
        def _(sp):
            sp.dma_start(idx_raw[:, :], idx_in).then_inc(idx_loaded, 16)
            sp.dma_start(idx_base[:, :], base_in).then_inc(idx_loaded, 16)
            sp.dma_start(neg[:, :], neg_in).then_inc(small_loaded, 16)
            sp.dma_start(b0[:, :], b0_in).then_inc(small_loaded, 16)
            sp.dma_start(b1[:, :], b1_in).then_inc(small_loaded, 16)
            sp.dma_start(sel0_raw, sel0_in).then_inc(sel_loaded, 16)
            sp.dma_start(sel1_raw, sel1_in).then_inc(sel_loaded, 16)
            turn_rows(0, 0)
            turn_rows(0, 1)
            sp.wait_ge(feat_clear, 1)
            sp.dma_start(feat[0:DENSE, 0, :], dense_in).then_inc(top_loaded, 16)
            sp.dma_start(wt1[0:DENSE, 0, :], wt1_in[S1 + HALF:S1 + HALF + DENSE, :]).then_inc(top_loaded, 16)
            sp.dma_start(wt1[HALF:128, 0, :], wt1_in[0:HALF, :]).then_inc(top_loaded, 16)
            sp.dma_start(wt1[:, 1, :], wt1_in[HALF:HALF + S1, :]).then_inc(top_loaded, 16)
            sp.dma_start(wt2[:, :, :], wt2_in.rearrange("(t p) n -> p t n", p=128)).then_inc(top_loaded, 16)
            sp.dma_start(wt3[:, :], wt3_in).then_inc(top_loaded, 16)
            sp.dma_start(bt1[:, :], bt1_in).then_inc(top_loaded, 16)
            sp.dma_start(bt2[:, :], bt2_in).then_inc(top_loaded, 16)
            for k in range(DMA_LEAD):
                if by_dma(k):
                    spread_by_dma(0, k)
            sync_body(0)
            with sp.Fori(1, BODIES - 1) as it:
                sync_body(it)
            sync_body(BODIES - 1, last=True)
            sp.wait_ge(top_act, N1 // 128 + N2 // 128 + 1)
            sp.dma_start(out, y[:, :]).then_inc(y_stored, 16)
            sp.wait_ge(y_stored, 16)

        @block.gpsimd
        def _(pool):
            pool.wait_ge(idx_loaded, 32)
            pool.tensor_tensor(idx[:, :], idx_raw[:, :], idx_base[:, :], ALU.add).then_inc(idx_ready, 1)
            pool.wait_ge(idx_ready, 1)
            for q in range(2):
                take_indices(0, q)
                for g in range(GATHERS):
                    fetch_rows(q, g)
            pool_body(0)
            with pool.Fori(1, BODIES - 1) as it:
                pool_body(it)
            pool_body(BODIES - 1, last=True)

        @block.scalar
        def _(act):
            act.dma_start(raw0[:, :], w0a_in).then_inc(w0_loaded, 16)
            act.dma_start(raw0b, w0b_in).then_inc(w0_loaded, 16)
            act.dma_start(raw1[:, :], w1_in).then_inc(w1_loaded, 16)
            act.wait_ge(sel_loaded, 32)
            act.activation(sel0[:, :, :].rearrange("p t m -> p (t m)"), sel0_raw,
                           ACT.Copy).then_inc(sel0_ready, 1)
            act.activation(sel1[:, :, :].rearrange("p t m -> p (t m)"), sel1_raw,
                           ACT.Copy).then_inc(sel1_ready, 1)
            split_x_high(0, 0)
            act.wait_ge(w0_sum, 1)
            act.activation(w0h[:, :, :].rearrange("p t m -> p (t m)"), raw0[:, :],
                           ACT.Copy).then_inc(w0_high, 1)
            act.wait_ge(w1_loaded, 16)
            act.activation(w1h[:, :, :].rearrange("p t m -> p (t m)"), raw1[:, :],
                           ACT.Copy).then_inc(w1_high, 1)
            split_x_high(0, 1)
            act.wait_ge(small_loaded, 48)
            finish_layer0(0, 0, steps(0, -1), None)
            scalar_body(0, first=True)
            with act.Fori(1, BODIES - 1) as it:
                scalar_body(it)
            scalar_body(BODIES - 1, last=True)
            act.wait_ge(top_loaded, 8 * 16)
            for m in range(N1 // 128):
                act.wait_ge(top_mm, m + 1)
                act.activation(a1[:, m, :], spread[:, m // 2, m % 2, :], ACT.Relu,
                               bias=bt1[:, m:m + 1]).then_inc(top_act, 1)
            for m in range(N2 // 128):
                act.wait_ge(top_mm, N1 // 128 + m + 1)
                act.activation(a2[:, m, :], acc1[:, m, :], ACT.Relu, bias=bt2[:, m:m + 1]).then_inc(top_act, 1)
            act.wait_ge(top_mm, N1 // 128 + N2 // 128 + 1)
            act.activation(y[:, :], acc0[:, 0:B // 128], ACT.Copy).then_inc(top_act, 1)

        @block.vector
        def _(dve):
            dve.memset(feat[:, :, :], 0.0)
            dve.memset(wt1[:, 0, :], 0.0).then_inc(feat_clear, 1)
            dve.wait_ge(w0_loaded, 32)
            dve.tensor_tensor(raw0[:, :], raw0[:, :], raw0b, ALU.add).then_inc(w0_sum, 1)
            dve.wait_ge(small_loaded, 48)
            split_x(0, 0)
            for s in range(PRE):
                multiply(0, s - PRE, PRE_KINDS[s])
            split_x(0, 1)
            dve.wait_ge(w0_high, 1)
            dve.tensor_tensor(w0l[:, :, :].rearrange("p t m -> p (t m)"), raw0[:, :],
                              w0h[:, :, :].rearrange("p t m -> p (t m)").bitcast(f32),
                              ALU.subtract).then_inc(w0_ready, 1)
            dve.wait_ge(w1_high, 1)
            dve.tensor_tensor(w1l[:, :, :].rearrange("p t m -> p (t m)"), raw1[:, :],
                              w1h[:, :, :].rearrange("p t m -> p (t m)").bitcast(f32),
                              ALU.subtract).then_inc(w1_ready, 1)
            vector_body(0, first=True)
            with dve.Fori(1, BODIES - 1) as it:
                vector_body(it)
            vector_body(BODIES - 1, last=True)

        @block.tensor
        def _(pe):
            pe.wait_ge(sel0_ready, 1)
            for s in range(NR):
                spread_x(0, s - PRE, PRE_KINDS[s])
            pe.wait_ge(w0_sum, 1)
            pe.wait_ge(sel1_ready, 1)
            for s in range(PRE):
                ahead = s - PRE + NR
                spread_x(0, ahead, PRE_KINDS[s + NR] if ahead < 0 else None)
                contract(0, s - PRE, PRE_KINDS[s])
            pe.wait_ge(w0_ready, 1)
            for k in range(NR, LEAD):
                spread_x(0, k)
            pe.wait_ge(w1_ready, 1)
            tensor_body(0)
            with pe.Fori(1, BODIES - 1) as it:
                tensor_body(it)
            tensor_body(BODIES - 1, last=True)
            pe.wait_ge(top_loaded, 8 * 16)
            pe.wait_ge(sum0_done, CHUNKS)
            for m in range(N1 // 128):
                pe.matmul(spread[:, m // 2, m % 2, :], wt1[:, 0, m * 128:(m + 1) * 128], feat[:, 0, :],
                          start=True, stop=False)
            pe.wait_ge(sum1_done, CHUNKS)
            for m in range(N1 // 128):
                pe.matmul(spread[:, m // 2, m % 2, :], wt1[:, 1, m * 128:(m + 1) * 128], feat[:, 1, :],
                          start=False, stop=True).then_inc(top_mm, 1)
            for t in range(N1 // 128):
                pe.wait_ge(top_act, t + 1)
                for m in range(N2 // 128):
                    mm = pe.matmul(acc1[:, m, :], wt2[:, t, m * 128:(m + 1) * 128], a1[:, t, :],
                                   start=(t == 0), stop=(t == N1 // 128 - 1))
                    if t == N1 // 128 - 1:
                        mm.then_inc(top_mm, 1)
            pe.wait_ge(top_act, N1 // 128 + N2 // 128)
            for g in range(B // 128):
                for t in range(N2 // 128):
                    mm = pe.matmul(acc0[:, g:g + 1], a2[:, t, g * 128:(g + 1) * 128], wt3[:, t:t + 1],
                                   start=(t == 0), stop=(t == N2 // 128 - 1))
            mm.then_inc(top_mm, 1)


def kernel(**inputs):
    import concourse.bacc as bacc
    from concourse.bass_utils import run_bass_kernel_spmd

    a = {k: np.asarray(v) for k, v in inputs.items()}
    tables = [a[f"tbl_{f}"] for f in range(F)]
    starts = np.concatenate([[0], np.cumsum([t.shape[0] for t in tables])])[:F].astype(np.int32)
    ids = a["ids"].reshape(CHUNKS, CB, GATHERS, FG).transpose(3, 1, 0, 2).reshape(128, CHUNKS * GATHERS)
    base = np.broadcast_to(starts.reshape(1, 1, GATHERS, FG), (CHUNKS, CB, GATHERS, FG))
    base = base.transpose(3, 1, 0, 2).reshape(128, CHUNKS * GATHERS)
    dist = np.arange(3 * T0)
    rot = (np.arange(F)[None, :] + dist[:, None]) % F
    field0 = rot.reshape(T0 * K0)
    field1 = np.repeat(np.arange(F), HALF)
    hot = lambda f: np.tile((f[None, :] == np.arange(F)[:, None]), (2, 1)).astype(np.float32)
    w0 = a["L0_rec_W0"]
    i = np.arange(F)[None, :].repeat(3 * T0, 0)
    w0a = w0[i, rot]
    w0b = w0[rot, i].copy()
    w0b[0] = 0
    w0b[F // 2] = 0
    tiled = lambda w: w.reshape(T0, K0, S0).transpose(1, 0, 2).reshape(K0, T0 * S0)
    w1 = a["L0_rec_W1"].reshape(T1, 128, S1).transpose(1, 0, 2).reshape(128, T1 * S1)
    arrays = {
        "idx": ids, "idx_base": base, "table": np.concatenate(tables, 0),
        "sel0": hot(field0), "sel1": hot(field1), "w0a": tiled(w0a), "w0b": tiled(w0b), "w1": w1,
        "b0": a["L0_rec_b0"].reshape(S0, 1), "b1": a["L0_rec_b1"].reshape(S1, 1),
        "neg": np.repeat(np.float32([0, -1]), F).reshape(SPLIT, 1),
        "dense_t": a["dense_ctx"].T, "w_top1": a["W_top1"], "b_top1": a["b_top1"].reshape(-1, 128).T,
        "w_top2": a["W_top2"], "b_top2": a["b_top2"].reshape(-1, 128).T,
        "w_top3": a["W_top3"].reshape(-1, 128).T,
    }
    nc = bacc.Bacc("TRN2", target_bir_lowering=False, num_devices=1)
    args = []
    for name, value in arrays.items():
        arrays[name] = value = np.ascontiguousarray(value)
        args.append(nc.dram_tensor(f"{name}_dram", value.shape, mybir.dt.from_np(value.dtype), kind="ExternalInput").ap())
    out = nc.dram_tensor("y_out", (128, B // 128), mybir.dt.float32, kind="ExternalOutput").ap()
    build(nc, *args, out)
    result = run_bass_kernel_spmd(nc, [{f"{n}_dram": v for n, v in arrays.items()}], core_ids=[0])
    return np.ascontiguousarray(result.results[0]["y_out"].T).reshape(B, 1)
```
